# Optimizing a Trainium2 kernel written in Bass

```python
import numpy as np
import jax
import jax.numpy as jnp

def _softmax(x, axis=-1):
    return jax.nn.softmax(x, axis=axis)

def _gelu(x):
    return jax.nn.gelu(x, approximate=True)

def _silu(x):
    return jax.nn.silu(x)

def _sigmoid(x):
    return jax.nn.sigmoid(x)

def _layernorm(x, axis=-1, eps=1e-05):
    m = jnp.mean(x, axis=axis, keepdims=True)
    v = jnp.var(x, axis=axis, keepdims=True)
    return (x - m) / jnp.sqrt(v + eps)

def _scatter_add(tgt, idx, src, axis=0):
    return tgt.at[idx].add(src)

def _segment_sum(src, seg, n):
    return jax.ops.segment_sum(src, seg, n)
kernel_name = 'mk_seq_postln_d2_jaxref_r8_cb8476'

def setup_inputs(seed: int=0):
    np.random.seed(seed)
    _w = jnp.asarray

    def _L0_attn_setup():
        import math
        import jax
        import jax.numpy as jnp
        import numpy as np
        from jax import lax
        B_, L, D_MODEL = (2, 128, 256)
        D_STATE, D_CONV, EXPAND = (16, 4, 2)
        D_INNER = EXPAND * D_MODEL
        DT_RANK = math.ceil(D_MODEL / 16)

        def _silu(v):
            return v * jax.nn.sigmoid(v)

        def _mamba_forward(hidden_states, in_proj_w, conv_w, conv_b, x_proj_w, dt_proj_w, dt_proj_b, A_log, D, out_proj_w):
            b, l, _ = hidden_states.shape
            xz = jnp.einsum('bld,ed->bel', hidden_states, in_proj_w)
            x, z = (xz[:, :D_INNER, :], xz[:, D_INNER:, :])
            A = -jnp.exp(A_log.astype(jnp.float32))
            xp = jnp.pad(x, ((0, 0), (0, 0), (D_CONV - 1, 0)))
            x = lax.conv_general_dilated(xp, conv_w[:, None, :], window_strides=(1,), padding='VALID', dimension_numbers=('NCH', 'OIH', 'NCH'), feature_group_count=D_INNER)
            x = _silu(x + conv_b[None, :, None])
            x_dbl = jnp.einsum('bdl,kd->blk', x, x_proj_w)
            dt_lo = x_dbl[..., :DT_RANK]
            Bmat = x_dbl[..., DT_RANK:DT_RANK + D_STATE]
            Cmat = x_dbl[..., DT_RANK + D_STATE:]
            delta = jax.nn.softplus(jnp.einsum('blr,dr->bld', dt_lo, dt_proj_w) + dt_proj_b.astype(jnp.float32))
            xt = jnp.transpose(x, (2, 0, 1))
            dl = jnp.transpose(delta, (1, 0, 2))
            Bl = jnp.transpose(Bmat, (1, 0, 2))
            Cl = jnp.transpose(Cmat, (1, 0, 2))

            def step(h, inp):
                d_t, B_t, C_t, x_t = inp
                dA = jnp.exp(d_t[..., None] * A)
                h = h * dA + d_t[..., None] * B_t[:, None, :] * x_t[..., None]
                y_t = jnp.sum(h * C_t[:, None, :], axis=-1)
                return (h, y_t)
            h0 = jnp.zeros((b, D_INNER, D_STATE), jnp.float32)
            _, ys = lax.scan(step, h0, (dl, Bl, Cl, xt))
            y = jnp.transpose(ys, (1, 0, 2))
            y = y + jnp.transpose(x, (0, 2, 1)) * D[None, None, :]
            y = y * _silu(jnp.transpose(z, (0, 2, 1)))
            out = jnp.einsum('bld,ed->ble', y, out_proj_w)
            return out
        key = jax.random.key(seed)
        ks = jax.random.split(key, 8)
        hidden_states = jax.random.normal(ks[0], (B_, L, D_MODEL), jnp.float32)
        in_proj_w = jax.random.normal(ks[1], (2 * D_INNER, D_MODEL), jnp.float32) * D_MODEL ** (-0.5)
        conv_w = jax.random.normal(ks[2], (D_INNER, D_CONV), jnp.float32) * D_CONV ** (-0.5)
        conv_b = jnp.zeros((D_INNER,), jnp.float32)
        x_proj_w = jax.random.normal(ks[3], (DT_RANK + 2 * D_STATE, D_INNER), jnp.float32) * D_INNER ** (-0.5)
        dt_std = DT_RANK ** (-0.5)
        dt_proj_w = jax.random.uniform(ks[4], (D_INNER, DT_RANK), jnp.float32, minval=-dt_std, maxval=dt_std)
        dt = jnp.exp(jax.random.uniform(ks[5], (D_INNER,), jnp.float32) * (math.log(0.1) - math.log(0.001)) + math.log(0.001))
        dt = jnp.clip(dt, 0.0001)
        dt_proj_b = dt + jnp.log(-jnp.expm1(-dt))
        A_log = jnp.log(jnp.broadcast_to(jnp.arange(1, D_STATE + 1, dtype=jnp.float32), (D_INNER, D_STATE)))
        D = jnp.ones((D_INNER,), jnp.float32)
        out_proj_w = jax.random.normal(ks[6], (D_MODEL, D_INNER), jnp.float32) * D_INNER ** (-0.5)
        return {'hidden_states': hidden_states, 'in_proj_w': in_proj_w, 'conv_w': conv_w, 'conv_b': conv_b, 'x_proj_w': x_proj_w, 'dt_proj_w': dt_proj_w, 'dt_proj_b': dt_proj_b, 'A_log': A_log, 'D': D, 'out_proj_w': out_proj_w}
    _L0_attn_in = _L0_attn_setup()

    def _L0_ffn_setup():
        import jax, jax.numpy as jnp
        import numpy as np
        TOP_K = 4

        def _silu_and_mul(gu):
            g, u = jnp.split(gu, 2, axis=-1)
            return jax.nn.silu(g) * u
        key = jax.random.key(seed)
        ks = jax.random.split(key, 7)
        H, E, I, Is = (256, 16, 176, 704)
        s = 0.02
        return {'hidden_states': jax.random.normal(ks[0], (4, 128, H), dtype=jnp.float32), 'gate_w': jax.random.normal(ks[1], (E, H), dtype=jnp.float32) * s, 'sgate_w': jax.random.normal(ks[2], (1, H), dtype=jnp.float32) * s, 'w13': jax.random.normal(ks[3], (E, 2 * I, H), dtype=jnp.float32) * s, 'w2': jax.random.normal(ks[4], (E, H, I), dtype=jnp.float32) * s, 'shared_gate_up_w': jax.random.normal(ks[5], (2 * Is, H), dtype=jnp.float32) * s, 'shared_down_w': jax.random.normal(ks[6], (H, Is), dtype=jnp.float32) * s}
    _L0_ffn_in = _L0_ffn_setup()

    def _L1_attn_setup():
        import jax, jax.numpy as jnp
        import numpy as np
        BATCH, SEQ, EMBED, STATE = (4, 256, 256, 16)
        key = jax.random.key(seed)
        ks = jax.random.split(key, 8)
        s = 0.02
        return {'x': jax.random.normal(ks[0], (BATCH, SEQ, EMBED), jnp.float32), 'proj_in_w': jax.random.normal(ks[1], (EMBED, EMBED), jnp.float32) * s, 'proj_in_b': jnp.zeros((EMBED,), jnp.float32), 'proj_out_w': jax.random.normal(ks[2], (EMBED, EMBED), jnp.float32) * s, 'proj_out_b': jnp.zeros((EMBED,), jnp.float32), 'A': jax.random.normal(ks[3], (EMBED, STATE), jnp.float32) * 0.01, 'B_w': jax.random.normal(ks[4], (STATE, EMBED), jnp.float32) * s, 'C_w': jax.random.normal(ks[5], (EMBED, STATE), jnp.float32) * s, 'D_param': jnp.ones((EMBED,), jnp.float32)}
    _L1_attn_in = _L1_attn_setup()

    def _L1_ffn_setup():
        import jax, jax.numpy as jnp
        import numpy as np
        NUM_EXPERTS = 8
        TOP_K = 2
        EMB = 256
        MLP = 512
        B, S = (4, 128)
        key = jax.random.key(seed)
        ks = jax.random.split(key, 5)
        scale_x = 1.0
        return {'x': jax.random.normal(ks[0], (B, S, EMB), dtype=jnp.float32), 'gate_kernel': jax.random.normal(ks[1], (EMB, NUM_EXPERTS), dtype=jnp.float32) / np.sqrt(EMB), 'w0_kernel': jax.random.normal(ks[2], (NUM_EXPERTS, EMB, MLP), dtype=jnp.float32) / np.sqrt(EMB), 'w1_kernel': jax.random.normal(ks[3], (NUM_EXPERTS, EMB, MLP), dtype=jnp.float32) / np.sqrt(EMB), 'wo_kernel': jax.random.normal(ks[4], (NUM_EXPERTS, MLP, EMB), dtype=jnp.float32) / np.sqrt(MLP)}
    _L1_ffn_in = _L1_ffn_setup()
    _d = {'L0_attn_hidden_states': _L0_attn_in['hidden_states'], 'L0_attn_in_proj_w': _L0_attn_in['in_proj_w'], 'L0_attn_conv_w': _L0_attn_in['conv_w'], 'L0_attn_conv_b': _L0_attn_in['conv_b'], 'L0_attn_x_proj_w': _L0_attn_in['x_proj_w'], 'L0_attn_dt_proj_w': _L0_attn_in['dt_proj_w'], 'L0_attn_dt_proj_b': _L0_attn_in['dt_proj_b'], 'L0_attn_A_log': _L0_attn_in['A_log'], 'L0_attn_D': _L0_attn_in['D'], 'L0_attn_out_proj_w': _L0_attn_in['out_proj_w'], 'L0_ffn_gate_w': _L0_ffn_in['gate_w'], 'L0_ffn_sgate_w': _L0_ffn_in['sgate_w'], 'L0_ffn_w13': _L0_ffn_in['w13'], 'L0_ffn_w2': _L0_ffn_in['w2'], 'L0_ffn_shared_gate_up_w': _L0_ffn_in['shared_gate_up_w'], 'L0_ffn_shared_down_w': _L0_ffn_in['shared_down_w'], 'L1_attn_proj_in_w': _L1_attn_in['proj_in_w'], 'L1_attn_proj_in_b': _L1_attn_in['proj_in_b'], 'L1_attn_proj_out_w': _L1_attn_in['proj_out_w'], 'L1_attn_proj_out_b': _L1_attn_in['proj_out_b'], 'L1_attn_A': _L1_attn_in['A'], 'L1_attn_B_w': _L1_attn_in['B_w'], 'L1_attn_C_w': _L1_attn_in['C_w'], 'L1_attn_D_param': _L1_attn_in['D_param'], 'L1_ffn_gate_kernel': _L1_ffn_in['gate_kernel'], 'L1_ffn_w0_kernel': _L1_ffn_in['w0_kernel'], 'L1_ffn_w1_kernel': _L1_ffn_in['w1_kernel'], 'L1_ffn_wo_kernel': _L1_ffn_in['wo_kernel']}
    _x0 = _d['L0_attn_hidden_states']
    _d['L0_attn_hidden_states'] = jax.random.normal(jax.random.fold_in(jax.random.key(seed), 1), (8, 512, 256), dtype=_x0.dtype)
    del _x0
    return _d

def reference(L0_attn_hidden_states, L0_attn_in_proj_w, L0_attn_conv_w, L0_attn_conv_b, L0_attn_x_proj_w, L0_attn_dt_proj_w, L0_attn_dt_proj_b, L0_attn_A_log, L0_attn_D, L0_attn_out_proj_w, L0_ffn_gate_w, L0_ffn_sgate_w, L0_ffn_w13, L0_ffn_w2, L0_ffn_shared_gate_up_w, L0_ffn_shared_down_w, L1_attn_proj_in_w, L1_attn_proj_in_b, L1_attn_proj_out_w, L1_attn_proj_out_b, L1_attn_A, L1_attn_B_w, L1_attn_C_w, L1_attn_D_param, L1_ffn_gate_kernel, L1_ffn_w0_kernel, L1_ffn_w1_kernel, L1_ffn_wo_kernel):

    def _L0_attn_ref(hidden_states, in_proj_w, conv_w, conv_b, x_proj_w, dt_proj_w, dt_proj_b, A_log, D, out_proj_w):
        import math
        import jax
        import jax.numpy as jnp
        import numpy as np
        from jax import lax
        B_, L, D_MODEL = (2, 128, 256)
        D_STATE, D_CONV, EXPAND = (16, 4, 2)
        D_INNER = EXPAND * D_MODEL
        DT_RANK = math.ceil(D_MODEL / 16)

        def _silu(v):
            return v * jax.nn.sigmoid(v)

        def _mamba_forward(hidden_states, in_proj_w, conv_w, conv_b, x_proj_w, dt_proj_w, dt_proj_b, A_log, D, out_proj_w):
            b, l, _ = hidden_states.shape
            xz = jnp.einsum('bld,ed->bel', hidden_states, in_proj_w)
            x, z = (xz[:, :D_INNER, :], xz[:, D_INNER:, :])
            A = -jnp.exp(A_log.astype(jnp.float32))
            xp = jnp.pad(x, ((0, 0), (0, 0), (D_CONV - 1, 0)))
            x = lax.conv_general_dilated(xp, conv_w[:, None, :], window_strides=(1,), padding='VALID', dimension_numbers=('NCH', 'OIH', 'NCH'), feature_group_count=D_INNER)
            x = _silu(x + conv_b[None, :, None])
            x_dbl = jnp.einsum('bdl,kd->blk', x, x_proj_w)
            dt_lo = x_dbl[..., :DT_RANK]
            Bmat = x_dbl[..., DT_RANK:DT_RANK + D_STATE]
            Cmat = x_dbl[..., DT_RANK + D_STATE:]
            delta = jax.nn.softplus(jnp.einsum('blr,dr->bld', dt_lo, dt_proj_w) + dt_proj_b.astype(jnp.float32))
            xt = jnp.transpose(x, (2, 0, 1))
            dl = jnp.transpose(delta, (1, 0, 2))
            Bl = jnp.transpose(Bmat, (1, 0, 2))
            Cl = jnp.transpose(Cmat, (1, 0, 2))

            def step(h, inp):
                d_t, B_t, C_t, x_t = inp
                dA = jnp.exp(d_t[..., None] * A)
                h = h * dA + d_t[..., None] * B_t[:, None, :] * x_t[..., None]
                y_t = jnp.sum(h * C_t[:, None, :], axis=-1)
                return (h, y_t)
            h0 = jnp.zeros((b, D_INNER, D_STATE), jnp.float32)
            _, ys = lax.scan(step, h0, (dl, Bl, Cl, xt))
            y = jnp.transpose(ys, (1, 0, 2))
            y = y + jnp.transpose(x, (0, 2, 1)) * D[None, None, :]
            y = y * _silu(jnp.transpose(z, (0, 2, 1)))
            out = jnp.einsum('bld,ed->ble', y, out_proj_w)
            return out
        return _mamba_forward(hidden_states, in_proj_w, conv_w, conv_b, x_proj_w, dt_proj_w, dt_proj_b, A_log, D, out_proj_w)

    def _L0_ffn_ref(hidden_states, gate_w, sgate_w, w13, w2, shared_gate_up_w, shared_down_w):
        import jax, jax.numpy as jnp
        import numpy as np
        TOP_K = 4

        def _silu_and_mul(gu):
            g, u = jnp.split(gu, 2, axis=-1)
            return jax.nn.silu(g) * u
        B, S, H = hidden_states.shape
        x = hidden_states.reshape(-1, H)
        E = gate_w.shape[0]
        shared = _silu_and_mul(x @ shared_gate_up_w.T) @ shared_down_w.T
        shared = shared * jax.nn.sigmoid(x @ sgate_w.T)
        router_logits = x @ gate_w.T
        routing_weights = jax.nn.softmax(router_logits.astype(jnp.float32), axis=-1)
        topk_w, topk_ids = jax.lax.top_k(routing_weights, TOP_K)

        def body(acc, ew):
            w13_e, w2_e, e = ew
            coef = jnp.sum(jnp.where(topk_ids == e, topk_w, 0.0), axis=-1)
            h = _silu_and_mul(x @ w13_e.T)
            acc = acc + (h @ w2_e.T).astype(jnp.float32) * coef[:, None]
            return (acc, None)
        init = jnp.zeros((x.shape[0], H), dtype=jnp.float32)
        sparse_out, _ = jax.lax.scan(body, init, (w13, w2, jnp.arange(E)))
        out = shared + sparse_out.astype(x.dtype)
        return out.reshape(B, S, H)

    def _L1_attn_ref(x, proj_in_w, proj_in_b, proj_out_w, proj_out_b, A, B_w, C_w, D_param):
        import jax, jax.numpy as jnp
        import numpy as np
        BATCH, SEQ, EMBED, STATE = (4, 256, 256, 16)
        x_proj = x @ proj_in_w.T + proj_in_b
        delta = jax.nn.softplus(x_proj @ B_w.T)
        sigA = jax.nn.sigmoid(A)
        Bsz, L, D = x.shape
        S = A.shape[1]

        def step(h, inp):
            x_t, d_t = inp
            h = h * sigA + x_t[:, :, None] * d_t[:, None, :]
            y_t = h.sum(axis=1) @ C_w.T + D_param * x_t
            return (h, y_t)
        h0 = jnp.zeros((Bsz, D, S), x.dtype)
        xs = (jnp.swapaxes(x_proj, 0, 1), jnp.swapaxes(delta, 0, 1))
        _, ys = jax.lax.scan(step, h0, xs)
        y = jnp.swapaxes(ys, 0, 1)
        y = y @ proj_out_w.T + proj_out_b
        return y + x

    def _L1_ffn_ref(x, gate_kernel, w0_kernel, w1_kernel, wo_kernel):
        import jax, jax.numpy as jnp
        import numpy as np
        NUM_EXPERTS = 8
        TOP_K = 2
        EMB = 256
        MLP = 512
        B, S = (4, 128)
        gate_logits = jnp.einsum('bsd,de->bse', x, gate_kernel)
        top_k_weights, top_k_indices = jax.lax.top_k(gate_logits, TOP_K)
        top_k_weights = jax.nn.softmax(top_k_weights.astype(jnp.float32), axis=-1).astype(x.dtype)
        one_hot = jax.nn.one_hot(top_k_indices, NUM_EXPERTS, dtype=x.dtype)
        combine = jnp.einsum('bsk,bske->bse', top_k_weights, one_hot)
        h0 = jnp.einsum('bsd,edm->bsem', x, w0_kernel)
        h1 = jnp.einsum('bsd,edm->bsem', x, w1_kernel)
        inter = jax.nn.silu(h0) * h1
        out = jnp.einsum('bse,bsem,emd->bsd', combine, inter, wo_kernel)
        return out
    x = L0_attn_hidden_states
    x = _layernorm(x + _L0_attn_ref(x, L0_attn_in_proj_w, L0_attn_conv_w, L0_attn_conv_b, L0_attn_x_proj_w, L0_attn_dt_proj_w, L0_attn_dt_proj_b, L0_attn_A_log, L0_attn_D, L0_attn_out_proj_w), axis=-1)
    x = _layernorm(x + _L0_ffn_ref(x, L0_ffn_gate_w, L0_ffn_sgate_w, L0_ffn_w13, L0_ffn_w2, L0_ffn_shared_gate_up_w, L0_ffn_shared_down_w), axis=-1)
    x = _layernorm(x + _L1_attn_ref(x, L1_attn_proj_in_w, L1_attn_proj_in_b, L1_attn_proj_out_w, L1_attn_proj_out_b, L1_attn_A, L1_attn_B_w, L1_attn_C_w, L1_attn_D_param), axis=-1)
    x = _layernorm(x + _L1_ffn_ref(x, L1_ffn_gate_kernel, L1_ffn_w0_kernel, L1_ffn_w1_kernel, L1_ffn_wo_kernel), axis=-1)
    return x

_drawn_inputs = setup_inputs


def setup_inputs(seed=0):
    import zlib

    import numpy as np

    out = dict(_drawn_inputs(seed))
    spreads = {'L0_attn_conv_b': (0.0, 0.1),
     'L0_attn_D': (1.0, 0.2),
     'L1_attn_proj_in_b': (0.0, 0.1),
     'L1_attn_proj_out_b': (0.0, 0.1),
     'L1_attn_D_param': (1.0, 0.2)}
    factors = {'L0_ffn_gate_w': 5.844,
     'L0_ffn_sgate_w': 16.945,
     'L0_ffn_w13': 5.585,
     'L0_ffn_w2': 5.18,
     'L1_attn_A': 35.828,
     'L1_attn_B_w': 4.054}
    for name, (base, spread) in spreads.items():
        noise = np.random.default_rng([zlib.crc32(name.encode()), seed]).standard_normal(out[name].shape)
        drawn = base * np.exp(spread * noise) if base else spread * noise
        out[name] = jnp.asarray(drawn.astype(out[name].dtype))
    for name, factor in factors.items():
        out[name] = (out[name] * factor).astype(out[name].dtype)
    return out
```

```python
from contextlib import ExitStack

import numpy as np

import concourse.bass as bass
from concourse import mybir

F32 = mybir.dt.float32
BF16 = mybir.dt.bfloat16
ALU = mybir.AluOpType
ACT = mybir.ActivationFunctionType
AX = mybir.AxisListType

P = 128
BATCH, L, D = 8, 512, 256
KD = D // P
DI, CONV, NST, RANK = 512, 4, 16, 16
CB = DI // P
XD = RANK + 2 * NST
E0, K0, I0, IS = 16, 4, 176, 704
E1, K1, I1 = 8, 2, 512
T0 = -(-(E0 * I0 + IS) // P)
T1 = E1 * I1 // P
TILES = (T0, T1)
TW = 4 * P + D
EPS = 1e-5

NS = 2
GROUPS = NST // NS
UM = GROUPS * CB
US = GROUPS * KD
YF = UM // 2
BC_RING, DA_RING, H_RING, W_RING = 4, 2, 4, 4
EPART = 32

PARAMS = [("w_in", KD * 2 * DI), ("w_x", CB * XD), ("w_out", CB * D), ("w_dt", DI), ("c_w", D),
          ("w_pin", KD * D), ("w_pout", KD * D), ("w_b", KD * NST), ("gate0", KD * (E0 + 1)),
          ("gate1", KD * E1), ("ident", P), ("onecol", 2 * NST - 1), ("conv_w", CB * CONV),
          ("conv_b", CB), ("dt_b", CB), ("a_log", CB * NST), ("d_m", CB), ("b_pin", KD),
          ("b_pout", KD), ("a_s", KD * NST), ("d_s", KD), ("before", E0 * E0)]
OFF, NPAR = {}, 0
for _name, _n in PARAMS:
    OFF[_name] = (NPAR, NPAR + _n)
    NPAR += _n

M_X, M_XP, M_DT = 0, CB, CB + 1
M_Z = M_DT + CB
M_Y = M_Z + CB
M_OUT = M_Y + YF
M_MEAN = M_OUT + KD
M_VAR = M_MEAN + 1
NM = M_VAR + 1
S_XP, S_DL, S_H, S_YC, S_PO, S_MEAN, S_VAR = 0, KD, KD + 1, KD + 2, 2 * KD + 2, 3 * KD + 2, 3 * KD + 3
NSF = S_VAR + 1
C_EXTRA = 4


def mixer_unit(u):
    return 2 * (u // (2 * CB)) + u % 2, (u // 2) % CB


def build(nc, xT, params, sel, ffn_w, out):
    with ExitStack() as ctx:
        def sb(name, shape, dt=F32):
            return ctx.enter_context(nc.sbuf_tensor(name, shape, dt))

        def ps(name, shape):
            return ctx.enter_context(nc.psum_tensor(name, shape, F32))

        def sem(name):
            return ctx.enter_context(nc.semaphore(name))

        par = sb("par", [P, NPAR])

        def cols(name, **dims):
            a, b = OFF[name]
            v = par[:, a:b]
            return v.rearrange("p (a b) -> p a b", **dims) if dims else v

        w_in, w_x, w_out = cols("w_in", a=KD), cols("w_x", a=CB), cols("w_out", a=CB)
        w_dt, c_w = cols("w_dt"), cols("c_w")
        w_pin, w_pout, w_b = cols("w_pin", a=KD), cols("w_pout", a=KD), cols("w_b", a=KD)
        gates = (cols("gate0", a=KD), cols("gate1", a=KD))
        ident, onecol, conv_w = cols("ident"), cols("onecol"), cols("conv_w", a=CB)
        conv_b, dt_b, a_log, d_m = cols("conv_b"), cols("dt_b"), cols("a_log", a=CB), cols("d_m")
        b_pin, b_pout, a_s, d_s = cols("b_pin"), cols("b_pout"), cols("a_s", a=KD), cols("d_s")
        before = cols("before", a=E0)
        sel_sb = sb("sel_sb", [3 * EPART, T0 + E1, P], BF16)
        mean_w = sb("mean_w", [P, P])
        eps_b = sb("eps_b", [P, 1])
        neg_a = sb("neg_a", [P, CB, NST])
        decay = sb("decay", [P, KD, NST])
        half_cw = sb("half_cw", [P, CB, CONV])
        half_cb = sb("half_cb", [P, CB])

        x_in = sb("x_in", [P, KD, L])
        x_pad = sb("x_pad", [P, 2, CONV - 1 + L])
        half_x = sb("half_x", [P, 2, L])
        tanh_m = sb("tanh_m", [P, 2, L])
        xu = sb("xu", [P, CB, L])
        delta = sb("delta", [P, CB, L])
        y = sb("y", [P, CB, L])
        z_act = sb("z_act", [P, CB, L])
        x_dbl = sb("x_dbl", [XD, L])
        b_bc = sb("b_bc", [P, BC_RING, NS, L])
        c_bc = sb("c_bc", [P, BC_RING, NS, L])
        d_a = sb("d_a", [P, DA_RING, NS, L])
        h_buf = sb("h_buf", [P, H_RING, NS, L])
        pre = sb("pre", [P, KD, L])
        sq = sb("sq", [P, KD, L])
        rstd = sb("rstd", [P, L])
        xp, ys = y[:, 0:KD], y[:, KD:2 * KD]
        sp_v, sp_a, sp_d, h_sum = (z_act[0:NST, i] for i in range(4))
        xs = [sb(f"x{i}", [P, KD, L]) for i in (1, 2, 3)]
        w_ring = sb("w_ring", [P, W_RING, TW])
        tanh_g = sb("tanh_g", [P, 2, L])
        gated_u = sb("gated_u", [P, 2, L])
        hid = sb("hid", [P, 2, L])
        pre_f = sb("pre_f", [P, KD, L])
        sq_f = sb("sq_f", [P, KD, L])
        rstd_f = sb("rstd_f", [P, L])
        coef_parts = sb("coef_parts", [3 * EPART, L], BF16)
        rest = sb("rest", [E0 + 1, L])
        mid = sb("mid", [E0 + 1, L], BF16)
        TT = L // P
        logits = sb("logits", [P, TT, E0 + 1])
        prob = sb("prob", [P, TT, E0 + 1])
        coef = sb("coef", [P, TT, E0 + 1])
        rank = sb("rank", [P, TT, E0])
        top = sb("top", [P, TT])
        inv = sb("inv", [P, TT])
        greater, equal = pre_f, sq_f

        gate_ps = [ps(f"gate_ps{i}", [P, L]) for i in range(2)]
        up_ps = [ps(f"up_ps{i}", [P, L]) for i in range(2)]
        side_ps = ps("side_ps", [P, L])
        out_ps = [ps(f"out_ps{i}", [P, L]) for i in range(KD)]
        mix_ps = ps("mix_ps", [P, L])

        bc_dram = nc.dram_tensor("bc_scratch", [2 * NST, L], F32, kind="Internal").ap()
        dl_dram = nc.dram_tensor("dl_scratch", [NST, L], F32, kind="Internal").ap()

        par_loaded = sem("par_loaded")
        prep_act = sem("prep_act")
        prep_dve = sem("prep_dve")
        prep_pool = sem("prep_pool")
        act_step, dve_step = sem("act_step"), sem("dve_step")
        x_loaded = sem("x_loaded")
        mix_filled, mix_drained = sem("mix_filled"), sem("mix_drained")
        conv_done, tanh_done, silu_done = sem("conv_done"), sem("tanh_done"), sem("silu_done")
        bc_stored, dl_stored = sem("bc_stored"), sem("dl_stored")
        b_loaded = [sem(f"b_loaded{i}") for i in range(BC_RING)]
        c_loaded = [sem(f"c_loaded{i}") for i in range(BC_RING)]
        softplus_log = sem("softplus_log")
        delta_done, u_done = sem("delta_done"), sem("u_done")
        da_done, bx_done, scanned, hc_done, reduced = (
            sem(n) for n in ("da_done", "bx_done", "scanned", "hc_done", "reduced"))
        y_gated = sem("y_gated")
        squared, rstd_done = sem("squared"), sem("rstd_done")
        x_ready = [sem(f"x{i}_ready") for i in (1, 2, 3)]
        s_log, s_delta, ssm_pre = sem("s_log"), sem("s_delta"), sem("ssm_pre")
        w_loaded = [sem(f"w_loaded{i}") for i in range(W_RING)]
        side_filled, side_drained = sem("side_filled"), sem("side_drained")
        shifted, prob_done, coef_done = sem("shifted"), sem("prob_done"), sem("coef_done")
        gu_filled, tanh_g_done, gu_drained = sem("gu_filled"), sem("tanh_g_done"), sem("gu_drained")
        tile_done = sem("tile_done")
        out_drained = sem("out_drained")
        squared_f, rstd_f_done = sem("squared_f"), sem("rstd_f_done")
        out_ready, out_stored = sem("out_ready"), sem("out_stored")

        def ffn_count(done, per_stage, extra=0):
            return done[0] * (T0 * per_stage + extra) + done[1] * (T1 * per_stage + extra)

        def drained_before(done):
            return done[0] * NM + done[1] * NSF

        def filled_before(done):
            return done[0] * (NM - YF) + done[1] * (NSF - 1)

        def units_before(done):
            return done[0] * UM + done[1] * US

        def m_filled(done, j):
            return filled_before(done) + (j + 1 if j < M_Y else j + 1 - YF)

        def s_filled(done, j):
            return filled_before(done) + (j + 1 if j < S_H else j)

        def waits_of(eng):
            def wait(*needs):
                counts = [n if isinstance(n, int) else eng.to_reg(n) for _, n in needs]
                for (signal, _), n in zip(needs, counts):
                    eng.wait_ge(signal, n)
            return wait

        ctx.enter_context(nc.allow_non_contiguous_dma(reason="rows sent to all partitions"))
        block = ctx.enter_context(nc.Block())

        @block.sync
        def _(sp):
            wait = waits_of(sp)
            sp.dma_start(par[:], params).then_inc(par_loaded, 16)
            sp.dma_start(sel_sb[:], sel).then_inc(par_loaded, 16)

            def load_x(b, at):
                sp.wait_ge(x_ready[0], b)
                sp.dma_start(x_in[:], xT[:, :, bass.ds(at, L)]).then_inc(x_loaded, 16)

            def load_rows(done, g, ssm):
                slot = g % BC_RING
                if ssm:
                    last = KD * (g - BC_RING) + KD
                    src = dl_dram
                    stored = (dl_stored, 16 * (done[1] + 1))
                else:
                    g0 = g - BC_RING
                    last = (g0 // 2) * 2 * CB + 2 * CB - 1 + g0 % 2
                    src = bc_dram[0:NST, :]
                    stored = (bc_stored, 16 * (done[0] + 1))
                wait(stored, (bx_done, units_before(done) + max(last, 0)))
                sp.dma_start(b_bc[:, slot], bass_rows(src, g)).then_inc(b_loaded[slot], 16)
                if not ssm:
                    sp.wait_ge(hc_done, done[0] * UM + max(last, 0))
                    sp.dma_start(c_bc[:, slot], bass_rows(bc_dram[NST:2 * NST, :], g)).then_inc(
                        c_loaded[slot], 16)

            def bass_rows(src, g):
                rows = src[g * NS:(g + 1) * NS, :].rearrange("n l -> (n l)")
                return rows.partition_broadcast(P)

            def load_weights(layer, done, t):
                sp.wait_ge(tile_done, ffn_count(done, 1) + max(t - W_RING + 1, 0))
                sp.dma_start(w_ring[:, t % W_RING], ffn_w[layer * T0 + t]).then_inc(
                    w_loaded[t % W_RING], 16)

            def store(b, at):
                sp.wait_ge(out_ready, b + 1)
                sp.dma_start(out[:, :, bass.ds(at, L)], pre_f[:]).then_inc(out_stored, 16)

            with sp.Fori(0, BATCH) as b:
                at = sp.snap(b * L)
                load_x(b, at)
                for g in range(GROUPS):
                    load_rows((b, b), g, False)
                for t in range(T0):
                    load_weights(0, (b, b), t)
                for g in range(GROUPS):
                    load_rows((b + 1, b), g, True)
                for t in range(T1):
                    load_weights(1, (b + 1, b), t)
                store(b, at)
            sp.wait_ge(out_stored, 16 * BATCH)

        @block.gpsimd
        def _(pool):
            nc.gpsimd.memset(mean_w[:], 1.0 / D)
            nc.gpsimd.memset(eps_b[:], EPS)
            nc.gpsimd.memset(x_pad[:, :, 0:CONV - 1], 0.0)
            nc.gpsimd.memset(d_a[:, :, :, 0:1], 0.0)
            nc.gpsimd.memset(coef_parts[:], 0.0).then_inc(prep_pool, 1)

            def scan_input(done, u, ssm):
                g, c = (u // KD, u % KD) if ssm else mixer_unit(u)
                src = xp[:, c:c + 1] if ssm else xu[:, c:c + 1]
                if u == 0:
                    if ssm:
                        pool.wait_ge(mix_drained, drained_before(done) + KD)
                    else:
                        pool.wait_ge(u_done, done[0] + 1)
                pool.wait_ge(b_loaded[g % BC_RING],
                             16 * (done[0] + done[1]) * (GROUPS // BC_RING) + 16 * (g // BC_RING + 1))
                pool.wait_ge(reduced, units_before(done) + max(u - H_RING + 1, 0))
                nc.gpsimd.tensor_tensor(h_buf[:, u % H_RING], src.to_broadcast([P, NS, L]),
                                        b_bc[:, g % BC_RING], ALU.mult).then_inc(bx_done, 1)

            def times_c(done, u):
                g, _ = mixer_unit(u)
                pool.wait_ge(scanned, units_before(done) + u + 1)
                pool.wait_ge(c_loaded[g % BC_RING],
                             16 * done[0] * (GROUPS // BC_RING) + 16 * (g // BC_RING + 1))
                h = h_buf[:, u % H_RING]
                nc.gpsimd.tensor_tensor(h, h, c_bc[:, g % BC_RING], ALU.mult).then_inc(hc_done, 1)

            with pool.Fori(0, BATCH) as b:
                for u in range(UM + 1):
                    if u < UM:
                        scan_input((b, b), u, False)
                    if u >= 1:
                        times_c((b, b), u - 1)
                for u in range(US):
                    scan_input((b + 1, b), u, True)

        @block.scalar
        def _(act):
            steps = [0, 0]

            def link(ins):
                steps[0] += 1
                ins.then_inc(act_step, 1)
                act.wait_ge(act_step, steps[1] * ACT_STEPS + steps[0])

            act.wait_ge(par_loaded, 32)
            nc.scalar.activation(neg_a[:], a_log, ACT.Exp).then_inc(prep_act, 1)
            nc.scalar.activation(decay[:], a_s, ACT.Exp, scale=-1.0).then_inc(prep_act, 1)
            act.wait_ge(prep_pool, 1)
            act.wait_ge(prep_dve, 1)

            def conv_input(done, m):
                act.wait_ge(mix_filled, m_filled(done, M_X + m))
                act.wait_ge(conv_done, done[0] * CB + max(m - 1, 0))
                nc.scalar.copy(x_pad[:, m % 2, CONV - 1:], mix_ps[:]).then_inc(mix_drained, 1)

            def conv_tanh(done, m):
                act.wait_ge(conv_done, done[0] * CB + m + 1)
                act.wait_ge(silu_done, done[0] * 2 * CB + max(m - 1, 0))
                nc.scalar.activation(tanh_m[:, m % 2], half_x[:, m % 2], ACT.Tanh).then_inc(tanh_done, 1)

            def rows_out(done):
                act.wait_ge(mix_filled, m_filled(done, M_XP))
                act.wait_ge(bc_stored, 16 * done[0])
                nc.scalar.copy(x_dbl[:], mix_ps[0:XD, :]).then_inc(mix_drained, 1)
                act.wait_ge(mix_drained, drained_before(done) + M_XP + 1)
                act.wait_ge(hc_done, done[0] * UM)
                act.dma_start(bc_dram, x_dbl[RANK:XD, :]).then_inc(bc_stored, 16)

            def delta_in(done, m):
                act.wait_ge(mix_filled, m_filled(done, M_DT + m))
                nc.scalar.activation(delta[:, m], mix_ps[:], ACT.Identity,
                                     bias=dt_b[:, m:m + 1]).then_inc(mix_drained, 1)

            def softplus(done):
                act.wait_ge(mix_drained, drained_before(done) + M_DT + CB)
                link(nc.scalar.activation(y[:], delta[:], ACT.Abs))
                link(nc.scalar.activation(y[:], y[:], ACT.Exp, scale=-1.0))
                nc.scalar.activation(y[:], y[:], ACT.Ln, bias=1.0).then_inc(softplus_log, 1)

            def z_in(done, m):
                act.wait_ge(mix_filled, m_filled(done, M_Z + m))
                act.wait_ge(silu_done, done[0] * 2 * CB + CB + m - 1)
                nc.scalar.activation(tanh_m[:, m % 2], mix_ps[:], ACT.Tanh, scale=0.5).then_inc(tanh_done, 1)
                nc.scalar.activation(z_act[:, m], mix_ps[:], ACT.Copy, scale=0.5).then_inc(mix_drained, 1)

            def decays(done, u):
                g, c = mixer_unit(u)
                if u == 0:
                    act.wait_ge(delta_done, done[0] + 1)
                act.wait_ge(scanned, units_before(done) + max(u - DA_RING + 1, 0))
                for j in range(NS):
                    last = nc.scalar.activation(d_a[:, u % DA_RING, j, 1:L], delta[:, c, 1:L], ACT.Exp,
                                                scale=neg_a[:, c, g * NS + j:g * NS + j + 1])
                last.then_inc(da_done, 1)

            def square(centered, n):
                act.wait_ge(mix_drained, n)
                nc.scalar.activation(sq[:], pre[:], ACT.Square).then_inc(squared, 1)

            def inv_std(filled):
                act.wait_ge(mix_filled, filled)
                nc.scalar.activation(rstd[:], mix_ps[:], ACT.Ln, bias=eps_b[:]).then_inc(mix_drained, 1)

            def inv_std_exp(n):
                act.wait_ge(mix_drained, n)
                nc.scalar.activation(rstd[:], rstd[:], ACT.Exp, scale=-0.5).then_inc(rstd_done, 1)

            def ssm_xp(done, m):
                act.wait_ge(mix_filled, s_filled(done, S_XP + m))
                nc.scalar.activation(xp[:, m], mix_ps[:], ACT.Identity,
                                     bias=b_pin[:, m:m + 1]).then_inc(mix_drained, 1)

            def ssm_delta(done):
                act.wait_ge(mix_filled, s_filled(done, S_DL))
                nc.scalar.copy(sp_v, mix_ps[0:NST, :]).then_inc(mix_drained, 1)
                act.wait_ge(mix_drained, drained_before(done) + S_DL + 1)
                link(nc.scalar.activation(sp_a, sp_v, ACT.Abs))
                link(nc.scalar.activation(sp_a, sp_a, ACT.Exp, scale=-1.0))
                nc.scalar.activation(sp_a, sp_a, ACT.Ln, bias=1.0).then_inc(s_log, 1)
                act.wait_ge(s_delta, done[1] + 1)
                act.wait_ge(bx_done, units_before(done))
                act.dma_start(dl_dram, sp_d).then_inc(dl_stored, 16)

            def ssm_sum(done):
                act.wait_ge(reduced, units_before(done) + US)
                nc.scalar.copy(h_sum, mix_ps[0:NST, :]).then_inc(mix_drained, 1)

            def ssm_out(done, m):
                act.wait_ge(mix_filled, s_filled(done, S_PO + m))
                nc.scalar.activation(pre[:, m], mix_ps[:], ACT.Identity,
                                     bias=b_pout[:, m:m + 1]).then_inc(mix_drained, 1)

            def router(layer, done):
                n = done[0] + done[1]
                e = E1 if layer else E0
                act.wait_ge(shifted, n + 1)
                if layer == 0:
                    nc.scalar.activation(prob[:, :, E0:], logits[:, :, E0:], ACT.Tanh, scale=0.5)
                nc.scalar.activation(prob[:, :, 0:e], coef[:, :, 0:e], ACT.Exp).then_inc(prob_done, 1)

            def gate_tanh(layer, done, t):
                n = ffn_count(done, 1) + t
                act.wait_ge(gu_filled, n + 1)
                act.wait_ge(gu_drained, ffn_count(done, 1) + max(t - 1, 0))
                nc.scalar.activation(tanh_g[:, t % 2], gate_ps[t % 2][:], ACT.Tanh,
                                     scale=0.5).then_inc(tanh_g_done, 1)

            def ffn_norm(layer, done):
                n = ffn_count(done, 1, C_EXTRA)
                t = TILES[layer]
                act.wait_ge(side_drained, n + t + 3)
                nc.scalar.activation(sq_f[:], pre_f[:], ACT.Square).then_inc(squared_f, 1)
                act.wait_ge(side_filled, n + t + 4)
                nc.scalar.activation(rstd_f[:], side_ps[:], ACT.Ln, bias=eps_b[:]).then_inc(side_drained, 1)
                act.wait_ge(side_drained, n + t + 4)
                nc.scalar.activation(rstd_f[:], rstd_f[:], ACT.Exp, scale=-0.5).then_inc(rstd_f_done, 1)

            def mamba(done):
                for m in range(CB):
                    conv_input(done, m)
                    conv_tanh(done, m)
                rows_out(done)
                for m in range(CB):
                    delta_in(done, m)
                softplus(done)
                for m in range(CB):
                    z_in(done, m)
                for u in range(UM):
                    decays(done, u)
                base = drained_before(done)
                square(pre, base + M_MEAN + 1)
                inv_std(m_filled(done, M_VAR))
                inv_std_exp(base + M_VAR + 1)

            def ssm(done):
                for m in range(KD):
                    ssm_xp(done, m)
                ssm_delta(done)
                ssm_sum(done)
                for m in range(KD):
                    ssm_out(done, m)
                base = drained_before(done)
                square(pre, base + S_MEAN + 1)
                inv_std(s_filled(done, S_VAR))
                inv_std_exp(base + S_VAR + 1)

            def ffn(layer, done):
                router(layer, done)
                for t in range(TILES[layer]):
                    gate_tanh(layer, done, t)
                ffn_norm(layer, done)

            with act.Fori(0, BATCH) as b:
                steps[1] = b
                mamba((b, b))
                ffn(0, (b, b))
                ssm((b + 1, b))
                ffn(1, (b + 1, b))
            assert steps[0] == ACT_STEPS, steps

        @block.vector
        def _(dve):
            steps = [0, 0]

            wait = waits_of(dve)

            def step(ins):
                steps[0] += 1
                ins.then_inc(dve_step, 1)
                return dve_step, steps[1] * DVE_STEPS + steps[0]

            def link(ins):
                wait(step(ins))

            dve.wait_ge(par_loaded, 32)
            nc.vector.tensor_scalar_mul(half_cw[:], conv_w, 0.5)
            nc.vector.tensor_scalar_mul(half_cb[:], conv_b, 0.5)
            dve.wait_ge(prep_act, 2)
            nc.vector.tensor_scalar_add(decay[:], decay[:], 1.0).then_inc(prep_dve, 1)
            dve.wait_ge(prep_dve, 1)
            nc.vector.reciprocal(decay[:], decay[:]).then_inc(prep_dve, 1)
            dve.wait_ge(prep_dve, 2)
            nc.vector.tensor_scalar_mul(neg_a[:], neg_a[:], -1.0).then_inc(prep_dve, 1)
            dve.wait_ge(prep_dve, 3)
            dve.wait_ge(prep_pool, 1)

            def convolve(done, m):
                wait((mix_drained, drained_before(done) + M_X + m + 1),
                     (tanh_done, done[0] * 2 * CB + max(m - 1, 0)))
                h, x = half_x[:, m % 2], x_pad[:, m % 2]
                link(nc.vector.tensor_scalar(h, x[:, CONV - 1:], half_cw[:, m, CONV - 1:], half_cb[:, m:m + 1],
                                             ALU.mult, ALU.add))
                for k in range(CONV - 2, -1, -1):
                    tap = nc.vector.scalar_tensor_tensor(h, x[:, k:k + L], half_cw[:, m, k:k + 1], h,
                                                         ALU.mult, ALU.add)
                    if k:
                        link(tap)
                tap.then_inc(conv_done, 1)

            def conv_silu(done, m):
                wait((conv_done, done[0] * CB + m + 1),
                     (tanh_done, done[0] * 2 * CB + m + 1))
                nc.vector.scalar_tensor_tensor(xu[:, m], tanh_m[:, m % 2], 1.0, half_x[:, m % 2],
                                               ALU.add, ALU.mult).then_inc(silu_done, 1)

            def delta_and_u(done):
                wait((softplus_log, done[0] + 1))
                nc.vector.scalar_tensor_tensor(delta[:].rearrange("p a l -> p (a l)"),
                                               delta[:].rearrange("p a l -> p (a l)"), 0.0,
                                               y[:].rearrange("p a l -> p (a l)"),
                                               ALU.max, ALU.add).then_inc(delta_done, 1)
                wait((delta_done, done[0] + 1),
                     (mix_filled, m_filled(done, M_XP)))
                for m in range(CB):
                    last = nc.vector.tensor_scalar(y[:, m], xu[:, m], d_m[:, m:m + 1], None, ALU.mult)
                link(last)
                nc.vector.tensor_tensor(xu[:], xu[:], delta[:], ALU.mult).then_inc(u_done, 1)

            def z_silu(done, m):
                wait((tanh_done, done[0] * 2 * CB + CB + m + 1),
                     (mix_drained, drained_before(done) + M_Z + m + 1))
                nc.vector.scalar_tensor_tensor(z_act[:, m], tanh_m[:, m % 2], 1.0, z_act[:, m],
                                               ALU.add, ALU.mult).then_inc(silu_done, 1)

            def scan(done, u, ssm):
                n = units_before(done) + u + 1
                h = h_buf[:, u % H_RING]
                if ssm:
                    wait((bx_done, n))
                    g, c = u // KD, u % KD
                    for j in range(NS):
                        s = g * NS + j
                        last = nc.vector.tensor_tensor_scan(h[:, j], decay[:, c, s:s + 1].to_broadcast([P, L]),
                                                            h[:, j], 0.0, ALU.mult, ALU.add)
                    last.then_inc(scanned, 1)
                    return
                wait((bx_done, n), (da_done, done[0] * UM + u + 1))
                flat = h.rearrange("p n l -> p (n l)")
                nc.vector.tensor_tensor_scan(flat, d_a[:, u % DA_RING].rearrange("p n l -> p (n l)"), flat,
                                             0.0, ALU.mult, ALU.add).then_inc(scanned, 1)

            def add_y(done, f):
                c = f % CB
                wait((reduced, units_before(done) + 2 * f + 2),
                     (mix_drained, drained_before(done) + M_Y + max(f - CB + 1, 0)))
                nc.vector.tensor_tensor(y[:, c], mix_ps[:], y[:, c], ALU.add).then_inc(mix_drained, 1)

            def gate_y(done):
                wait((mix_drained, drained_before(done) + M_Y + YF),
                     (silu_done, (done[0] + 1) * 2 * CB))
                nc.vector.tensor_tensor(y[:], y[:], z_act[:], ALU.mult).then_inc(y_gated, 1)

            def residual(done, m):
                wait((mix_filled, m_filled(done, M_OUT + m)))
                nc.vector.tensor_tensor(pre[:, m], mix_ps[:], x_in[:, m], ALU.add).then_inc(mix_drained, 1)

            def center(filled, *pre_ready):
                wait((mix_filled, filled), *pre_ready)
                nc.vector.tensor_tensor(pre[:], pre[:], mix_ps[:].rearrange("p (a l) -> p a l", a=1).to_broadcast(
                    [P, KD, L]), ALU.subtract).then_inc(mix_drained, 1)

            def scale_norm(dst, ready, n):
                wait((rstd_done, n))
                nc.vector.tensor_tensor(dst[:], pre[:], rstd[:].rearrange("p (a l) -> p a l", a=1).to_broadcast(
                    [P, KD, L]), ALU.mult).then_inc(ready, 1)

            def mamba(done):
                for m in range(CB):
                    convolve(done, m)
                    conv_silu(done, m)
                delta_and_u(done)
                for m in range(CB):
                    z_silu(done, m)
                for u in range(UM):
                    scan(done, u, False)
                    if u % 2 == 1 and u >= 3:
                        add_y(done, u // 2 - 1)
                add_y(done, YF - 1)
                gate_y(done)
                for m in range(KD):
                    residual(done, m)
                center(m_filled(done, M_MEAN), (mix_drained, drained_before(done) + M_OUT + KD))
                scale_norm(xs[0], x_ready[0], done[0] + done[1] + 1)

            def ssm(done):
                wait((s_log, done[1] + 1))
                nc.vector.scalar_tensor_tensor(sp_d, sp_v, 0.0, sp_a, ALU.max, ALU.add).then_inc(s_delta, 1)
                for u in range(US):
                    scan(done, u, True)
                for m in range(KD):
                    wait((mix_filled, s_filled(done, S_YC + m)))
                    nc.vector.scalar_tensor_tensor(ys[:, m], xp[:, m], d_s[:, m:m + 1], mix_ps[:],
                                                   ALU.mult, ALU.add).then_inc(mix_drained, 1)
                wait((mix_drained, drained_before(done) + S_PO + KD))
                nc.vector.scalar_tensor_tensor(pre[:].rearrange("p a l -> p (a l)"),
                                               xs[1][:].rearrange("p a l -> p (a l)"), 2.0,
                                               pre[:].rearrange("p a l -> p (a l)"),
                                               ALU.mult, ALU.add).then_inc(ssm_pre, 1)
                center(s_filled(done, S_MEAN), (ssm_pre, done[1] + 1))
                scale_norm(xs[2], x_ready[2], done[0] + done[1] + 1)

            def router(layer, done):
                n = done[0] + done[1]
                e, k = (E1, K1) if layer else (E0, K0)
                width = e if layer else e + 1
                side = ffn_count(done, 1, C_EXTRA)
                wait((side_filled, side + 1),
                     (out_stored, 16 * done[1]))
                nc.vector.tensor_copy(logits[:, :, 0:width], side_ps[:, 0:TT * width].rearrange(
                    "p (t e) -> p t e", t=TT)).then_inc(side_drained, 1)
                wait((side_drained, side + 1))
                lg = logits[:, :, 0:e]
                link(nc.vector.tensor_reduce(top[:], lg, AX.X, ALU.max))
                nc.vector.tensor_tensor(coef[:, :, 0:e], lg, top[:].rearrange("p (t a) -> p t a", a=1).to_broadcast(
                    [P, TT, e]), ALU.subtract).then_inc(shifted, 1)
                gt = greater[:].rearrange("p a l -> p (a l)")[:, 0:TT * e * e].rearrange(
                    "p (t i j) -> p t i j", t=TT, i=e)
                eq = equal[:].rearrange("p a l -> p (a l)")[:, 0:TT * e * e].rearrange(
                    "p (t i j) -> p t i j", t=TT, i=e)
                lj = lg.unsqueeze(2).to_broadcast([P, TT, e, e])
                li = lg.unsqueeze(3).to_broadcast([P, TT, e, e])
                lower = before[:, 0:e, 0:e].unsqueeze(1).to_broadcast([P, TT, e, e])
                nc.vector.tensor_tensor(gt, lj, li, ALU.is_gt)
                link(nc.vector.tensor_tensor(eq, lj, li, ALU.is_equal))
                link(nc.vector.tensor_tensor(eq, eq, lower, ALU.mult))
                link(nc.vector.tensor_tensor(gt, gt, eq, ALU.add))
                rk = rank[:, :, 0:e]
                ranked = step(nc.vector.tensor_reduce(rk, gt, AX.X, ALU.add))
                wait(ranked, (prob_done, n + 1))
                pr, cf = prob[:, :, 0:e], coef[:, :, 0:e]
                if layer == 0:
                    nc.vector.tensor_scalar(coef[:, :, E0:], prob[:, :, E0:], 0.25, 0.25, ALU.mult, ALU.add)
                link(nc.vector.scalar_tensor_tensor(cf, rk, float(k), pr, ALU.is_lt, ALU.mult))
                link(nc.vector.tensor_reduce(top[:], cf if layer else pr, AX.X, ALU.add))
                link(nc.vector.reciprocal(inv[:], top[:]))
                nc.vector.scalar_tensor_tensor(
                    cf, cf, 0.5, inv[:].rearrange("p (t a) -> p t a", a=1).to_broadcast([P, TT, e]),
                    ALU.mult, ALU.mult).then_inc(coef_done, 1)
                wait((side_filled, side + 2))
                hi, ct = coef_parts[0:width, :], side_ps[0:width, :]
                r, md = rest[0:width, :], mid[0:width, :]
                link(nc.vector.tensor_copy(hi, ct))
                link(nc.vector.tensor_tensor(r, ct, hi, ALU.subtract))
                link(nc.vector.tensor_copy(md, r))
                nc.vector.tensor_copy(coef_parts[EPART:EPART + width, :], md)
                nc.vector.tensor_tensor(coef_parts[2 * EPART:2 * EPART + width, :], r, md,
                                        ALU.subtract).then_inc(side_drained, 1)

            def gate_up(layer, done, t):
                n = ffn_count(done, 1) + t
                wait((tanh_g_done, n + 1))
                silu2 = tanh_g[:, t % 2]
                doubled = step(nc.vector.scalar_tensor_tensor(silu2, silu2, 1.0, gate_ps[t % 2][:],
                                                              ALU.add, ALU.mult))
                wait(doubled, (side_drained, ffn_count(done, 1, C_EXTRA) + 2 + max(t - 1, 0)))
                nc.vector.tensor_tensor(gated_u[:, t % 2], up_ps[t % 2][:], silu2, ALU.mult).then_inc(
                    gu_drained, 1)

            def weight_hidden(layer, done, t):
                wait((side_filled, ffn_count(done, 1, C_EXTRA) + 3 + t),
                     (gu_drained, ffn_count(done, 1) + t + 1),
                     (tile_done, ffn_count(done, 1) + max(t - 1, 0)))
                nc.vector.tensor_tensor(hid[:, t % 2], side_ps[:], gated_u[:, t % 2], ALU.mult).then_inc(
                    side_drained, 1)

            def ffn(layer, done):
                router(layer, done)
                tiles = TILES[layer]
                for t in range(tiles + 1):
                    if t < tiles:
                        gate_up(layer, done, t)
                    if t >= 1:
                        weight_hidden(layer, done, t - 1)
                x = xs[2 * layer]
                wait((tile_done, ffn_count(done, 1) + tiles))
                for m in range(KD):
                    last = nc.vector.tensor_tensor(pre_f[:, m], out_ps[m][:], x[:, m], ALU.add)
                last.then_inc(out_drained, 1)
                n = done[0] + done[1] + 1
                side = ffn_count(done, 1, C_EXTRA) + tiles
                wait((out_drained, n), (side_filled, side + 3))
                nc.vector.tensor_tensor(pre_f[:], pre_f[:], side_ps[:].rearrange("p (a l) -> p a l", a=1).to_broadcast(
                    [P, KD, L]), ALU.subtract).then_inc(side_drained, 1)
                wait((rstd_f_done, n))
                dst, ready = (pre_f, out_ready) if layer else (xs[1], x_ready[1])
                nc.vector.tensor_tensor(dst[:], pre_f[:], rstd_f[:].rearrange("p (a l) -> p a l", a=1).to_broadcast(
                    [P, KD, L]), ALU.mult).then_inc(ready, 1)

            with dve.Fori(0, BATCH) as b:
                steps[1] = b
                mamba((b, b))
                ffn(0, (b, b))
                ssm((b + 1, b))
                ffn(1, (b + 1, b))
            assert steps[0] == DVE_STEPS, steps

        @block.tensor
        def _(pe):
            pe.wait_ge(par_loaded, 32)
            pe.wait_ge(prep_pool, 1)

            def fill(base, j):
                pe.wait_ge(mix_drained, base + j)

            def project(w, lo, src, blocks, rows=P):
                for k in range(blocks):
                    last = nc.tensor.matmul(mix_ps[0:rows, :], w[:, k, lo:lo + rows], src[:, k],
                                            start=(k == 0), stop=(k == blocks - 1))
                return last

            def mean(src, bank):
                for k in range(KD):
                    last = nc.tensor.matmul(bank[:], mean_w[:], src[:, k], start=(k == 0), stop=(k == KD - 1))
                return last

            def mamba(done):
                base = drained_before(done)
                pe.wait_ge(x_loaded, 16 * (done[0] + 1))
                for m in range(CB):
                    fill(base, M_X + m)
                    project(w_in, m * P, x_in, KD).then_inc(mix_filled, 1)
                fill(base, M_XP)
                pe.wait_ge(silu_done, done[0] * 2 * CB + CB)
                project(w_x, 0, xu, CB, XD).then_inc(mix_filled, 1)
                for m in range(CB):
                    fill(base, M_DT + m)
                    nc.tensor.matmul(mix_ps[:], w_dt[0:RANK, m * P:(m + 1) * P], x_dbl[0:RANK, :],
                                     start=True, stop=True).then_inc(mix_filled, 1)
                for m in range(CB):
                    fill(base, M_Z + m)
                    project(w_in, DI + m * P, x_in, KD).then_inc(mix_filled, 1)
                for u in range(UM):
                    if u % 2 == 0:
                        fill(base, M_Y + u // 2)
                    pe.wait_ge(hc_done, done[0] * UM + u + 1)
                    for j in range(NS):
                        last = nc.tensor.matmul(mix_ps[:], ident, h_buf[:, u % H_RING, j],
                                                start=(u % 2 == 0 and j == 0), stop=(u % 2 == 1 and j == NS - 1))
                    last.then_inc(reduced, 1)
                pe.wait_ge(y_gated, done[0] + 1)
                for m in range(KD):
                    fill(base, M_OUT + m)
                    project(w_out, m * P, y, CB).then_inc(mix_filled, 1)
                fill(base, M_MEAN)
                mean(pre, mix_ps).then_inc(mix_filled, 1)
                fill(base, M_VAR)
                pe.wait_ge(squared, done[0] + done[1] + 1)
                mean(sq, mix_ps).then_inc(mix_filled, 1)

            def ssm(done):
                base = drained_before(done)
                pe.wait_ge(x_ready[1], done[1] + 1)
                for m in range(KD):
                    fill(base, S_XP + m)
                    project(w_pin, m * P, xs[1], KD).then_inc(mix_filled, 1)
                fill(base, S_DL)
                project(w_b, 0, xp, KD, NST).then_inc(mix_filled, 1)
                fill(base, S_H)
                for u in range(US):
                    pe.wait_ge(scanned, units_before(done) + u + 1)
                    for j in range(NS):
                        s = (u // KD) * NS + j
                        last = nc.tensor.matmul(mix_ps[0:NST, :], onecol[:, NST - 1 - s:2 * NST - 1 - s],
                                                h_buf[:, u % H_RING, j], start=(u == 0 and j == 0),
                                                stop=(u == US - 1 and j == NS - 1))
                    last.then_inc(reduced, 1)
                for m in range(KD):
                    fill(base, S_YC + m)
                    nc.tensor.matmul(mix_ps[:], c_w[0:NST, m * P:(m + 1) * P], h_sum,
                                     start=True, stop=True).then_inc(mix_filled, 1)
                for m in range(KD):
                    fill(base, S_PO + m)
                    project(w_pout, m * P, ys, KD).then_inc(mix_filled, 1)
                fill(base, S_MEAN)
                pe.wait_ge(ssm_pre, done[1] + 1)
                mean(pre, mix_ps).then_inc(mix_filled, 1)
                fill(base, S_VAR)
                pe.wait_ge(squared, done[0] + done[1] + 1)
                mean(sq, mix_ps).then_inc(mix_filled, 1)

            def down(layer, done, t):
                pe.wait_ge(side_drained, ffn_count(done, 1, C_EXTRA) + 3 + t)
                w = w_ring[:, t % W_RING, 4 * P:]
                for m in range(KD):
                    last = nc.tensor.matmul(out_ps[m][:], w[:, m * P:(m + 1) * P], hid[:, t % 2],
                                            start=(t == 0), stop=(t == TILES[layer] - 1))
                last.then_inc(tile_done, 1)

            def spread_coef(layer, done, t):
                pe.wait_ge(side_drained, ffn_count(done, 1, C_EXTRA) + 2 + t)
                which = T0 + t // (I1 // P) if layer else t
                nc.tensor.matmul(side_ps[:], sel_sb[:, which], coef_parts[:], start=True,
                                 stop=True).then_inc(side_filled, 1)

            def ffn(layer, done):
                x = xs[2 * layer]
                side = ffn_count(done, 1, C_EXTRA)
                tiles = TILES[layer]
                width = E1 if layer else E0 + 1
                pe.wait_ge(x_ready[2 * layer], done[layer] + 1)
                pe.wait_ge(side_drained, side)
                for tt in range(TT):
                    for k in range(KD):
                        last = nc.tensor.matmul(side_ps[:, tt * width:(tt + 1) * width],
                                                x[:, k, tt * P:(tt + 1) * P], gates[layer][:, k],
                                                start=(k == 0), stop=(k == KD - 1))
                last.then_inc(side_filled, 1)
                pe.wait_ge(coef_done, done[0] + done[1] + 1)
                pe.wait_ge(side_drained, side + 1)
                for tt in range(TT):
                    last = nc.tensor.matmul(side_ps[0:width, tt * P:(tt + 1) * P], coef[:, tt, 0:width], ident,
                                            start=True, stop=True)
                last.then_inc(side_filled, 1)
                pe.wait_ge(out_drained, done[0] + done[1])
                per_slot = (T0 // W_RING, T1 // W_RING)
                for t in range(tiles):
                    pe.wait_ge(w_loaded[t % W_RING], 16 * (done[0] * per_slot[0] + done[1] * per_slot[1])
                               + 16 * (t // W_RING + 1))
                    pe.wait_ge(gu_drained, ffn_count(done, 1) + max(t - 1, 0))
                    w = w_ring[:, t % W_RING]
                    for which, bank in ((0, gate_ps[t % 2]), (1, up_ps[t % 2])):
                        for k in range(KD):
                            lo = (which * KD + k) * P
                            last = nc.tensor.matmul(bank[:], w[:, lo:lo + P], x[:, k], start=(k == 0),
                                                    stop=(k == KD - 1))
                    last.then_inc(gu_filled, 1)
                    if t >= 1:
                        down(layer, done, t - 1)
                    spread_coef(layer, done, t)
                down(layer, done, tiles - 1)
                pe.wait_ge(out_drained, done[0] + done[1] + 1)
                mean(pre_f, side_ps).then_inc(side_filled, 1)
                pe.wait_ge(side_drained, side + tiles + 3)
                pe.wait_ge(squared_f, done[0] + done[1] + 1)
                mean(sq_f, side_ps).then_inc(side_filled, 1)

            with pe.Fori(0, BATCH) as b:
                mamba((b, b))
                ffn(0, (b, b))
                ssm((b + 1, b))
                ffn(1, (b + 1, b))


ACT_STEPS = 4
DVE_STEPS = 95


def kernel(**inputs):
    import concourse.bacc as bacc
    from concourse.bass_utils import run_bass_kernel_spmd

    a = {k: np.asarray(v) for k, v in inputs.items()}

    def rows(w, blocks):
        n = w.shape[0] // blocks
        return np.ascontiguousarray(w.reshape(blocks, n, -1).transpose(1, 0, 2)).reshape(n, -1)

    def padded(w):
        full = np.zeros((P, w.shape[1]), w.dtype)
        full[:w.shape[0]] = w
        return full

    onecol = np.zeros((P, 2 * NST - 1), np.float32)
    onecol[:, NST - 1] = 1.0
    before = np.broadcast_to(np.tril(np.ones((E0, E0), np.float32), -1).reshape(1, -1), (P, E0 * E0))
    gate0 = np.concatenate([a["L0_ffn_gate_w"], a["L0_ffn_sgate_w"]], 0).T
    values = {
        "w_in": rows(a["L0_attn_in_proj_w"].T, KD), "w_x": rows(a["L0_attn_x_proj_w"].T, CB),
        "w_out": rows(a["L0_attn_out_proj_w"].T, CB), "w_dt": padded(a["L0_attn_dt_proj_w"].T),
        "c_w": padded(a["L1_attn_C_w"].T), "w_pin": rows(a["L1_attn_proj_in_w"].T, KD),
        "w_pout": rows(a["L1_attn_proj_out_w"].T, KD), "w_b": rows(a["L1_attn_B_w"].T, KD),
        "gate0": rows(gate0, KD), "gate1": rows(a["L1_ffn_gate_kernel"], KD),
        "ident": np.eye(P, dtype=np.float32), "onecol": onecol, "conv_w": rows(a["L0_attn_conv_w"], CB),
        "conv_b": rows(a["L0_attn_conv_b"][:, None], CB), "dt_b": rows(a["L0_attn_dt_proj_b"][:, None], CB),
        "a_log": rows(a["L0_attn_A_log"], CB), "d_m": rows(a["L0_attn_D"][:, None], CB),
        "b_pin": rows(a["L1_attn_proj_in_b"][:, None], KD), "b_pout": rows(a["L1_attn_proj_out_b"][:, None], KD),
        "a_s": rows(a["L1_attn_A"], KD), "d_s": rows(a["L1_attn_D_param"][:, None], KD), "before": before,
    }
    params = np.concatenate([values[name] for name, _ in PARAMS], 1)

    def hidden_tiles(gate, up, dn, tiles):
        pad = tiles * P - gate.shape[1]
        g, u = (np.pad(w, ((0, 0), (0, pad))).reshape(KD, P, tiles, P).transpose(2, 1, 0, 3).reshape(
            tiles, P, KD * P) for w in (gate, up))
        return np.concatenate([g, u, np.pad(dn, ((0, pad), (0, 0))).reshape(tiles, P, D)], 2)

    w13, w2 = a["L0_ffn_w13"], a["L0_ffn_w2"]
    sgu, sdn = a["L0_ffn_shared_gate_up_w"], a["L0_ffn_shared_down_w"]
    ffn0 = hidden_tiles(np.concatenate([w13[:, :I0].reshape(-1, D), sgu[:IS]], 0).T,
                        np.concatenate([w13[:, I0:].reshape(-1, D), sgu[IS:]], 0).T,
                        np.concatenate([w2.transpose(0, 2, 1).reshape(-1, D), sdn.T], 0), T0)
    ffn1 = hidden_tiles(a["L1_ffn_w0_kernel"].transpose(1, 0, 2).reshape(D, -1),
                        a["L1_ffn_w1_kernel"].transpose(1, 0, 2).reshape(D, -1),
                        a["L1_ffn_wo_kernel"].reshape(-1, D), T1)
    ffn_w = np.ascontiguousarray(np.concatenate([ffn0, ffn1], 0))

    sel = np.zeros((3 * EPART, T0 + E1, P), np.float32)
    for t in range(T0):
        for i in range(P):
            unit = t * P + i
            expert = unit // I0 if unit < E0 * I0 else E0
            sel[[expert, EPART + expert, 2 * EPART + expert], t, i] = 1.0
    for e in range(E1):
        sel[[e, EPART + e, 2 * EPART + e], T0 + e, :] = 1.0
    sel = sel.astype(mybir.dt.np(BF16))

    xT = np.ascontiguousarray(a["L0_attn_hidden_states"].reshape(BATCH * L, D).T)
    nc = bacc.Bacc("TRN2", target_bir_lowering=False, num_devices=1)
    x_d = nc.dram_tensor("xT", [D, BATCH * L], F32, kind="ExternalInput").ap()
    p_d = nc.dram_tensor("params", [P, NPAR], F32, kind="ExternalInput").ap()
    s_d = nc.dram_tensor("sel", list(sel.shape), BF16, kind="ExternalInput").ap()
    w_d = nc.dram_tensor("ffn_w", list(ffn_w.shape), F32, kind="ExternalInput").ap()
    o_d = nc.dram_tensor("outT", [D, BATCH * L], F32, kind="ExternalOutput").ap()
    build(nc, x_d.rearrange("(k p) n -> p k n", p=P), p_d, s_d, w_d, o_d.rearrange("(k p) n -> p k n", p=P))
    res = run_bass_kernel_spmd(nc, [{"xT": xT, "params": params, "sel": sel, "ffn_w": ffn_w}], core_ids=[0])
    return np.ascontiguousarray(res.results[0]["outT"].T).reshape(BATCH, L, D)
```

```python
from collections import namedtuple
from contextlib import ExitStack

import numpy as np

import concourse.bass as bass
from concourse import mybir

F32 = mybir.dt.float32
F32R = mybir.dt.float32r
BF16 = mybir.dt.bfloat16
ALU = mybir.AluOpType
ACT = mybir.ActivationFunctionType
AX = mybir.AxisListType

P = 128
BATCH, L, D = 8, 512, 256
KD = D // P
DI, CONV, NST, RANK = 512, 4, 16, 16
CB = DI // P
XD = RANK + 2 * NST
E0, K0, I0, IS = 16, 4, 176, 704
E1, K1, I1 = 8, 2, 512
T0 = -(-(E0 * I0 + IS) // P)
T1 = E1 * I1 // P
TILES = (T0, T1)
GU = 2 * D
SPLITS = (T0 + T1) // 2
EPS = 1e-5

NS = 2
GROUPS = NST // NS
UM = GROUPS * CB
US = GROUPS * KD
PS = US // KD
BC_RING, DA_RING, H_RING, W_RING = 4, 2, 4, 4
EPART = 32

PARAMS = [("w_in", KD * 2 * DI), ("w_x", CB * XD), ("w_out", CB * D), ("w_dt", DI), ("c_w", D),
          ("w_pin", KD * D), ("w_pout", KD * D), ("w_b", KD * NST), ("gate0", KD * (E0 + 1)),
          ("gate1", KD * E1), ("ident", P), ("onecol", 2 * NST - 1), ("conv_w", CB * CONV),
          ("conv_b", CB), ("dt_b", CB), ("a_log", CB * NST), ("d_m", CB), ("b_pin", KD),
          ("b_pout", KD), ("a_s", KD * NST), ("d_s", KD), ("before", E0 * E0)]
OFF, NPAR = {}, 0
for _name, _n in PARAMS:
    OFF[_name] = (NPAR, NPAR + _n)
    NPAR += _n

F_X, F_XP, F_DT = 0, CB, CB + 1
F_Z = F_DT + CB
NF = F_Z + CB
B_OUT, B_MEAN, B_VAR, NB = 0, KD, KD + 1, KD + 2
S_XP, S_DL, S_H, S_YC, S_PO, S_MEAN, S_VAR = 0, KD, KD + 1, KD + 2, 2 * KD + 2, 3 * KD + 2, 3 * KD + 3
NSF = S_VAR + 1
SSM_END, TAIL = 17, 4
C_EXTRA = 2
Y_LAG = 3
DVE_C = 4

Done = namedtuple("Done", "front back ssm f0 f1")


def mixer_unit(u):
    return 2 * (u // (2 * CB)) + u % 2, (u // 2) % CB


def on_dve(u):
    return u % DVE_C == DVE_C - 1


FRONT = ([("in", m) for m in range(CB + 1)] + [("x_proj", 0)] + [("dt", m) for m in range(CB)]
         + [("softplus", 0), ("z", 0), ("u_y", 0)] + [("z", m) for m in range(1, CB + 1)])
BACK = [("unit", u) for u in range(UM + Y_LAG)] + [("out", m) for m in range(KD + 1)] + [
    ("b_mean", 0), ("b_var", 0), ("b_norm", 0)]
SSM = ([("xp", m) for m in range(KD)] + [("s_delta", 0), ("s_plus", 0)] + [("s_unit", u) for u in range(US + 2)]
       + [("c_y", m) for m in range(KD)] + [("s_out", m) for m in range(KD)]
       + [("s_mean", 0), ("s_var", 0), ("s_norm", 0)])


def spread(tiles, *parts):
    plan = [[] for _ in range(tiles)]
    for d, pieces, lo, hi in parts:
        for i, (name, n) in enumerate(pieces):
            plan[lo + i * (hi - lo) // len(pieces)].append((d, name, n))
    return plan


class Steps:

    def __init__(self, per_row):
        self.per_row, self.base, self.n = per_row, 0, 0

    def loop(self, i):
        self.start, self.base, self.n = self.n, self.n + (i - 1) * self.per_row, 0

    def behind(self):
        assert self.n == self.per_row, self.n
        self.base, self.n = self.start + (BATCH - 3) * self.per_row, 0

    def next(self):
        self.n += 1
        return self.base + self.n


def build(nc, xT, params, sel, gu_w, down_w, out):
    with ExitStack() as ctx:
        def sb(name, shape, dt=F32):
            return ctx.enter_context(nc.sbuf_tensor(name, shape, dt))

        def ps(name, shape):
            return ctx.enter_context(nc.psum_tensor(name, shape, F32))

        def sem(name):
            return ctx.enter_context(nc.semaphore(name))

        par = sb("par", [P, NPAR])

        def cols(name, **dims):
            a, b = OFF[name]
            v = par[:, a:b]
            return v.rearrange("p (a b) -> p a b", **dims) if dims else v

        w_in, w_x, w_out = cols("w_in", a=KD), cols("w_x", a=CB), cols("w_out", a=CB)
        w_dt, c_w = cols("w_dt"), cols("c_w")
        w_pin, w_pout, w_b = cols("w_pin", a=KD), cols("w_pout", a=KD), cols("w_b", a=KD)
        gates = (cols("gate0", a=KD), cols("gate1", a=KD))
        ident, onecol, conv_w = cols("ident"), cols("onecol"), cols("conv_w", a=CB)
        conv_b, dt_b, a_log, d_m = cols("conv_b"), cols("dt_b"), cols("a_log", a=CB), cols("d_m")
        b_pin, b_pout, a_s, d_s = cols("b_pin"), cols("b_pout"), cols("a_s", a=KD), cols("d_s")
        before = cols("before", a=E0)
        sel_sb = sb("sel_sb", [3 * EPART, T0 + E1, P], BF16)
        mean_w = sb("mean_w", [P, P])
        eps_b = sb("eps_b", [P, 1])
        neg_a = sb("neg_a", [P, CB, NST])
        decay = sb("decay", [P, KD, NST])
        half_cw = sb("half_cw", [P, CB, CONV])
        half_cb = sb("half_cb", [P, CB])

        x_in = sb("x_in", [P, KD, L])
        x_pad = sb("x_pad", [P, 2, CONV - 1 + L])
        half_x = sb("half_x", [P, 2, L])
        tanh_m = sb("tanh_m", [P, 2, L])
        xu = sb("xu", [P, CB, L])
        delta = sb("delta", [P, CB, L])
        y = sb("y", [P, CB, L])
        z_act = sb("z_act", [P, CB, L])
        x_dbl = sb("x_dbl", [XD, L])
        b_bc = sb("b_bc", [P, BC_RING, NS, L])
        c_bc = sb("c_bc", [P, BC_RING, NS, L])
        d_a = sb("d_a", [P, DA_RING, NS, L])
        h_buf = sb("h_buf", [P, H_RING, NS, L])
        pre, sq, rstd = h_buf[:, 0], h_buf[:, 1], h_buf[:, 2, 0]
        assert NS == KD
        xp, ys = c_bc[:, 0], c_bc[:, 1]
        sp_v, sp_a, sp_d, h_sum = (c_bc[0:NST, 2 + i // NS, i % NS] for i in range(4))
        xs = [sb(f"x{i}", [P, KD, L]) for i in (1, 2, 3)]
        gu_ring = sb("gu_ring", [P, W_RING, 2, GU], F32R)
        down_ring = sb("down_ring", [P, W_RING, D])
        x_parts = sb("x_parts", [P, 2, KD, L], F32R)
        tanh_g = sb("tanh_g", [P, 2, L])
        gated_u = sb("gated_u", [P, 2, L])
        hid = sb("hid", [P, 2, L])
        pre_f = sb("pre_f", [P, KD, L])
        sq_f = sb("sq_f", [P, KD, L])
        rstd_f = sb("rstd_f", [P, L])
        coef_parts = sb("coef_parts", [3 * EPART, L], BF16)
        rest = sb("rest", [E0 + 1, L])
        mid = sb("mid", [E0 + 1, L], BF16)
        TT = L // P
        logits = sb("logits", [P, TT, E0 + 1])
        prob = sb("prob", [P, TT, E0 + 1])
        coef = sb("coef", [P, TT, E0 + 1])
        rank = sb("rank", [P, TT, E0])
        top = sb("top", [P, TT])
        inv = sb("inv", [P, TT])
        greater, equal = gated_u, hid
        raw = [a[:].rearrange("p a (b l) -> p a b l", b=1) for a in (pre_f, sq_f)]

        gate_ps = [ps(f"gate_ps{i}", [P, L]) for i in range(2)]
        up_ps = [ps(f"up_ps{i}", [P, L]) for i in range(2)]
        side_ps = ps("side_ps", [P, L])
        out_ps = [ps(f"out_ps{i}", [P, L]) for i in range(KD)]
        mix_ps = ps("mix_ps", [P, L])

        bc_dram = nc.dram_tensor("bc_scratch", [2 * NST, L], F32, kind="Internal").ap()
        gu_dram = nc.dram_tensor("gu_split", [T0 + T1, P, 2, GU], F32, kind="Internal").ap()
        dl_dram = nc.dram_tensor("dl_scratch", [NST, L], F32, kind="Internal").ap()

        par_loaded = sem("par_loaded")
        prep_act = sem("prep_act")
        prep_dve = sem("prep_dve")
        prep_pool = sem("prep_pool")
        act_step, dve_step = sem("act_step"), sem("dve_step")
        raw_loaded = [sem(f"raw_loaded{i}") for i in range(2)]
        w_high, w_low = sem("w_high"), sem("w_low")
        split_stored = [sem(f"split_stored{i}") for i in range(2)]
        x_high, x_low = sem("x_high"), sem("x_low")
        x_loaded = sem("x_loaded")
        mix_filled, mix_drained = sem("mix_filled"), sem("mix_drained")
        conv_done, tanh_done, silu_done = sem("conv_done"), sem("tanh_done"), sem("silu_done")
        bc_stored, dl_stored = sem("bc_stored"), sem("dl_stored")
        b_loaded = [sem(f"b_loaded{i}") for i in range(BC_RING)]
        c_loaded = [sem(f"c_loaded{i}") for i in range(BC_RING)]
        softplus_log = sem("softplus_log")
        delta_done, u_done = sem("delta_done"), sem("u_done")
        da_done, bx_done, scanned = sem("da_done"), sem("bx_done"), sem("scanned")
        hc_done, y_added = sem("hc_done"), sem("y_added")
        paired, reduced = sem("paired"), sem("reduced")
        y_gated = sem("y_gated")
        squared, rstd_done = sem("squared"), sem("rstd_done")
        x_ready = [sem(f"x{i}_ready") for i in (1, 2, 3)]
        s_log, s_delta, ssm_pre = sem("s_log"), sem("s_delta"), sem("ssm_pre")
        w_loaded = [sem(f"w_loaded{i}") for i in range(W_RING)]
        side_filled, side_drained = sem("side_filled"), sem("side_drained")
        shifted, prob_done, coef_done = sem("shifted"), sem("prob_done"), sem("coef_done")
        gu_filled, tanh_g_done, gu_drained = sem("gu_filled"), sem("tanh_g_done"), sem("gu_drained")
        tile_done = sem("tile_done")
        out_drained = sem("out_drained")
        norm_filled, norm_drained = sem("norm_filled"), sem("norm_drained")
        squared_f, rstd_f_done = sem("squared_f"), sem("rstd_f_done")
        out_ready, out_stored = sem("out_ready"), sem("out_stored")

        def ffn_count(d, per_tile, extra=0):
            return d.f0 * (T0 * per_tile + extra) + d.f1 * (T1 * per_tile + extra)

        def side_count(d):
            return ffn_count(d, 1, C_EXTRA)

        def drained(d, j=0):
            return d.front * NF + d.back * NB + d.ssm * NSF + j

        def filled(d, j, ssm=False):
            return d.front * NF + d.back * NB + d.ssm * (NSF - 1) + (j if ssm and j >= S_H else j + 1)

        def units(d, u=0):
            return d.back * UM + d.ssm * US + u

        def pool_c(d, u):
            return d.back * (UM - UM // DVE_C) + u + 1 - (u + 1) // DVE_C

        def count(n):
            if isinstance(n, int):
                return max(n, 0)
            assert n.min_val > 0, n
            return n

        def counts(eng, *values):
            return [n if isinstance(n, int) else eng.to_reg(n) for n in map(count, values)]

        def schedule(eng, piece, head=None, tile=None, norm=None, steps=None):
            def slot(layer, d, former, parts):
                if head:
                    head(layer, d, former)
                plan = spread(TILES[layer], *parts)
                for t in range(TILES[layer]):
                    if tile:
                        tile(layer, d, t)
                    for dd, name, n in plan[t]:
                        piece(dd, name, n)

            def alone(layer, d):
                if norm:
                    norm(layer, d)

            for name, n in FRONT:
                piece(Done(0, 0, 0, 0, 0), name, n)
            splits = [("split", j) for j in range(SPLITS + 1)]
            for k, (name, n) in enumerate(BACK):
                piece(Done(1, 0, 0, 0, 0), name, n)
                for what in splits[k:k + 1]:
                    piece(Done(1, 0, 0, 0, 0), *what)
            first, second = Done(2, 2, 0, 0, 0), Done(2, 2, 0, 1, 0)
            slot(0, first, None, [(Done(1, 1, 0, 0, 0), FRONT, 0, 7),
                                  (Done(2, 1, 0, 0, 0), BACK[:-1], 7, T0)])
            alone(0, first)
            piece(Done(2, 1, 0, 1, 0), *BACK[-1])
            slot(0, second, None, [(second, SSM, 0, SSM_END), (second._replace(ssm=1), FRONT, SSM_END, T0)])

            def ffn1_and_scan(i):
                d = Done(i + 2, i + 1, i, i + 1, i - 1)
                slot(1, d, (0, d._replace(f0=i)), [(d, BACK[:UM + Y_LAG], 0, T1 - TAIL),
                                                   (d, BACK[UM + Y_LAG:], T1 - TAIL, T1)])

            def ffn0_and_ssm(i, front):
                d = Done(i + 2, i + 2, i, i + 1, i)
                slot(0, d, (1, d._replace(f1=i - 1)), [(d, SSM, 0, SSM_END),
                                                       (d._replace(ssm=i + 1), front, SSM_END, T0)])

            with eng.Fori(1, BATCH - 2) as i:
                if steps:
                    steps.loop(i)
                ffn1_and_scan(i)
                ffn0_and_ssm(i, FRONT)
            if steps:
                steps.behind()
            ffn1_and_scan(BATCH - 2)
            d = Done(BATCH, BATCH, BATCH - 2, BATCH - 1, BATCH - 2)
            slot(0, d, (1, d._replace(f1=BATCH - 3)), [(d, SSM, 0, T0)])
            d = Done(BATCH, BATCH, BATCH - 1, BATCH, BATCH - 2)
            slot(1, d, (0, d._replace(f0=BATCH - 1)), [(d, SSM[:-1], 0, T1)])
            alone(1, d)
            d = d._replace(f1=BATCH - 1)
            piece(d, *SSM[-1])
            slot(1, d, None, [])
            alone(1, d)

        ctx.enter_context(nc.allow_non_contiguous_dma(reason="rows sent to all partitions"))
        block = ctx.enter_context(nc.Block())

        @block.sync
        def _(sp):
            sp.dma_start(par[:], params).then_inc(par_loaded, 16)
            sp.dma_start(sel_sb[:], sel).then_inc(par_loaded, 16)

            def load_x(d):
                at = d.front * L
                if not isinstance(at, int):
                    at = sp.snap(at)
                sp.wait_ge(x_ready[0], count(d.back))
                sp.dma_start(x_in[:], xT[:, :, bass.ds(at, L)]).then_inc(x_loaded, 16)

            def rows_of(src, g):
                rows = src[g * NS:(g + 1) * NS, :].rearrange("n l -> (n l)")
                return rows.partition_broadcast(P)

            def load_bc(d, g):
                slot, former = g % BC_RING, g - BC_RING
                used = 0 if former < 0 else (former // 2) * 2 * CB + 2 * CB - 1 + former % 2
                bc_stored_n, bx_done_n = counts(sp, 16 * (d.back + 1), units(d, used))
                sp.wait_ge(bc_stored, bc_stored_n)
                sp.wait_ge(bx_done, bx_done_n)
                sp.dma_start(b_bc[:, slot], rows_of(bc_dram[0:NST, :], g)).then_inc(b_loaded[slot], 16)
                x_ready_n, y_added_n = counts(sp, d.ssm, d.back * UM + used)
                sp.wait_ge(x_ready[2], x_ready_n)
                sp.wait_ge(y_added, y_added_n)
                sp.dma_start(c_bc[:, slot], rows_of(bc_dram[NST:2 * NST, :], g)).then_inc(c_loaded[slot], 16)

            def load_delta(d, g):
                slot, former = g % BC_RING, g - BC_RING
                dl_stored_n, bx_done_n = counts(sp, 16 * (d.ssm + 1), units(d, max(KD * (former + 1), 0)))
                sp.wait_ge(dl_stored, dl_stored_n)
                sp.wait_ge(bx_done, bx_done_n)
                sp.dma_start(b_bc[:, slot], rows_of(dl_dram, g)).then_inc(b_loaded[slot], 16)

            def load_weights(layer, d, t):
                sp.wait_ge(tile_done, count(ffn_count(d, 1) + t - W_RING + 1))
                slot = t % W_RING
                sp.dma_start(gu_ring[:, slot].bitcast(F32), gu_dram[layer * T0 + t]).then_inc(w_loaded[slot], 16)
                sp.dma_start(down_ring[:, slot], down_w[layer * T0 + t]).then_inc(w_loaded[slot], 16)

            def load_raw(j):
                sp.wait_ge(w_low, count(j - 1))
                sp.dma_start(raw[j % 2], gu_w[2 * j:2 * j + 2].rearrange("t p (b l) -> p t b l", b=1)).then_inc(
                    raw_loaded[j % 2], 16)

            def store_split(j):
                sp.wait_ge(w_low, j + 1)
                half = j % 2
                sp.dma_start(gu_dram[2 * j:2 * j + 2].rearrange("t p h n -> p t h n"),
                             gu_ring[:, 2 * half:2 * half + 2].bitcast(F32)).then_inc(split_stored[half], 16)

            def store(d):
                at = d.f1 * L
                if not isinstance(at, int):
                    at = sp.snap(at)
                sp.wait_ge(out_ready, count(d.f1 + 1))
                sp.dma_start(out[:, :, bass.ds(at, L)], pre_f[:]).then_inc(out_stored, 16)

            def piece(d, name, n):
                if (name, n) == ("in", 0):
                    load_x(d)
                elif name == "split":
                    if n < SPLITS:
                        load_raw(n)
                    if n >= 1:
                        store_split(n - 1)
                elif (name, n) == ("z", CB):
                    for g in range(BC_RING):
                        load_bc(d, g)
                elif name == "unit" and n in (2 * CB + Y_LAG - 1, 4 * CB + Y_LAG - 1):
                    g = BC_RING + 2 * (n // (2 * CB) - 1)
                    load_bc(d, g)
                    load_bc(d, g + 1)
                elif name == "s_unit" and n == 0:
                    for g in range(BC_RING):
                        load_delta(d, g)
                elif name == "s_unit" and n % KD == 1 and n > KD and BC_RING + n // KD - 1 < GROUPS:
                    load_delta(d, BC_RING + n // KD - 1)

            def head(layer, d, former):
                if isinstance(d.f0, int) and d.f0 == 0:
                    for half in range(2):
                        sp.wait_ge(split_stored[half], 16 * (SPLITS // 2))
                for t in range(W_RING - 1):
                    load_weights(layer, d, t)
                if former and former[0]:
                    store(former[1])

            def tile(layer, d, t):
                if t + W_RING - 1 < TILES[layer]:
                    load_weights(layer, d, t + W_RING - 1)

            def norm(layer, d):
                if layer:
                    store(d)

            schedule(sp, piece, head, tile, norm)
            sp.wait_ge(out_stored, 16 * (BATCH + 1))

        @block.gpsimd
        def _(pool):
            nc.gpsimd.memset(mean_w[:], 1.0 / D)
            nc.gpsimd.memset(eps_b[:], EPS).then_inc(out_stored, 16)
            nc.gpsimd.memset(x_pad[:, :, 0:CONV - 1], 0.0)
            nc.gpsimd.memset(d_a[:, :, :, 0:1], 0.0)
            nc.gpsimd.memset(coef_parts[:], 0.0).then_inc(prep_pool, 1)

            def scan_input(d, u, ssm):
                g, c = (u // KD, u % KD) if ssm else mixer_unit(u)
                src = xp[:, c:c + 1] if ssm else xu[:, c:c + 1]
                if u == 0:
                    if ssm:
                        pool.wait_ge(mix_drained, count(drained(d, KD)))
                        pool.wait_ge(y_added, count(d.back * UM))
                        pool.wait_ge(x_ready[0], count(d.back))
                    else:
                        pool.wait_ge(u_done, count(d.back + 1))
                        pool.wait_ge(reduced, count(d.ssm * PS))
                        pool.wait_ge(x_ready[2], count(d.ssm))
                pool.wait_ge(b_loaded[g % BC_RING],
                             count(16 * ((d.back + d.ssm) * (GROUPS // BC_RING) + g // BC_RING + 1)))
                if ssm:
                    pool.wait_ge(reduced, count(d.ssm * PS + u // KD - 1))
                else:
                    pool.wait_ge(y_added, count(d.back * UM + u - H_RING + 1))
                nc.gpsimd.tensor_tensor(h_buf[:, u % H_RING], src.to_broadcast([P, NS, L]),
                                        b_bc[:, g % BC_RING], ALU.mult).then_inc(bx_done, 1)

            def times_c(d, u):
                g, _ = mixer_unit(u)
                pool.wait_ge(scanned, count(units(d, u + 1)))
                pool.wait_ge(c_loaded[g % BC_RING], count(16 * (d.back * (GROUPS // BC_RING) + g // BC_RING + 1)))
                h = h_buf[:, u % H_RING]
                nc.gpsimd.tensor_tensor(h, h, c_bc[:, g % BC_RING], ALU.mult).then_inc(hc_done, 1)

            def piece(d, name, n):
                if name == "unit":
                    if n < UM:
                        scan_input(d, n, False)
                    if 1 <= n <= UM and not on_dve(n - 1):
                        times_c(d, n - 1)
                elif name == "s_unit" and n < US:
                    scan_input(d, n, True)

            schedule(pool, piece)

        @block.scalar
        def _(act):
            steps = Steps(ACT_STEPS)

            def link(ins):
                ins.then_inc(act_step, 1)
                act.wait_ge(act_step, count(steps.next()))

            act.wait_ge(par_loaded, 32)
            nc.scalar.activation(neg_a[:], a_log, ACT.Exp).then_inc(prep_act, 1)
            nc.scalar.activation(decay[:], a_s, ACT.Exp, scale=-1.0).then_inc(prep_act, 1)
            act.wait_ge(prep_pool, 1)
            act.wait_ge(prep_dve, 3)

            def conv_input(d, m):
                act.wait_ge(mix_filled, count(filled(d, F_X + m)))
                act.wait_ge(conv_done, count(d.front * CB + m - 1))
                nc.scalar.copy(x_pad[:, m % 2, CONV - 1:], mix_ps[:]).then_inc(mix_drained, 1)

            def conv_tanh(d, m):
                act.wait_ge(conv_done, count(d.front * CB + m + 1))
                act.wait_ge(silu_done, count(d.front * 2 * CB + m - 1))
                nc.scalar.activation(tanh_m[:, m % 2], half_x[:, m % 2], ACT.Tanh).then_inc(tanh_done, 1)

            def rows_out(d):
                act.wait_ge(mix_filled, count(filled(d, F_XP)))
                act.wait_ge(bc_stored, count(16 * d.front))
                nc.scalar.copy(x_dbl[:], mix_ps[0:XD, :]).then_inc(mix_drained, 1)
                act.wait_ge(mix_drained, count(drained(d, F_XP + 1)))
                act.wait_ge(y_added, count(d.back * UM))
                act.dma_start(bc_dram, x_dbl[RANK:XD, :]).then_inc(bc_stored, 16)

            def delta_in(d, m):
                act.wait_ge(mix_filled, count(filled(d, F_DT + m)))
                act.wait_ge(da_done, count(d.back * UM))
                nc.scalar.activation(delta[:, m], mix_ps[:], ACT.Identity,
                                     bias=dt_b[:, m:m + 1]).then_inc(mix_drained, 1)

            def softplus(d):
                act.wait_ge(mix_drained, count(drained(d, F_DT + CB)))
                link(nc.scalar.activation(y[:], delta[:], ACT.Abs))
                link(nc.scalar.activation(y[:], y[:], ACT.Exp, scale=-1.0))
                nc.scalar.activation(y[:], y[:], ACT.Ln, bias=1.0).then_inc(softplus_log, 1)

            def z_in(d, m):
                act.wait_ge(mix_filled, count(filled(d, F_Z + m)))
                act.wait_ge(silu_done, count(d.front * 2 * CB + CB + m - 1))
                nc.scalar.activation(tanh_m[:, m % 2], mix_ps[:], ACT.Tanh, scale=0.5).then_inc(tanh_done, 1)
                nc.scalar.activation(z_act[:, m], mix_ps[:], ACT.Copy, scale=0.5).then_inc(mix_drained, 1)

            def decays(d, u):
                g, c = mixer_unit(u)
                act.wait_ge(delta_done, count(d.back + 1))
                act.wait_ge(scanned, count(units(d, u - DA_RING + 1)))
                for j in range(NS):
                    last = nc.scalar.activation(d_a[:, u % DA_RING, j, 1:L], delta[:, c, 1:L], ACT.Exp,
                                                scale=neg_a[:, c, g * NS + j:g * NS + j + 1])
                last.then_inc(da_done, 1)

            def square(centered):
                act.wait_ge(mix_drained, count(centered))
                nc.scalar.activation(sq, pre, ACT.Square).then_inc(squared, 1)

            def inv_std(variance, n):
                act.wait_ge(mix_filled, count(variance))
                nc.scalar.activation(rstd, mix_ps[:], ACT.Ln, bias=eps_b[:]).then_inc(mix_drained, 1)
                act.wait_ge(mix_drained, count(n))
                nc.scalar.activation(rstd, rstd, ACT.Exp, scale=-0.5).then_inc(rstd_done, 1)

            def ssm_delta(d):
                act.wait_ge(mix_filled, count(filled(d, S_DL)))
                nc.scalar.copy(sp_v, mix_ps[0:NST, :]).then_inc(mix_drained, 1)
                act.wait_ge(mix_drained, count(drained(d, S_DL + 1)))
                link(nc.scalar.activation(sp_a, sp_v, ACT.Abs))
                link(nc.scalar.activation(sp_a, sp_a, ACT.Exp, scale=-1.0))
                nc.scalar.activation(sp_a, sp_a, ACT.Ln, bias=1.0).then_inc(s_log, 1)

            def split_high(j):
                act.wait_ge(raw_loaded[j % 2], 16 * (j // 2 + 1))
                act.wait_ge(split_stored[j % 2], 16 * (j // 2))
                half = 2 * (j % 2)
                nc.scalar.activation(gu_ring[:, half:half + 2, 0:1], raw[j % 2], ACT.Copy).then_inc(w_high, 1)

            def piece(d, name, n):
                if name == "split" and n < SPLITS:
                    split_high(n)
                elif name == "in":
                    if n < CB:
                        conv_input(d, n)
                    if n >= 1:
                        conv_tanh(d, n - 1)
                elif name == "x_proj":
                    rows_out(d)
                elif name == "dt":
                    delta_in(d, n)
                elif name == "softplus":
                    softplus(d)
                elif name == "z" and n < CB:
                    z_in(d, n)
                elif name == "unit" and n < UM:
                    decays(d, n)
                elif name == "b_mean":
                    square(drained(d, B_MEAN + 1))
                elif name == "b_var":
                    inv_std(filled(d, B_VAR), drained(d, B_VAR + 1))
                elif name == "xp":
                    act.wait_ge(mix_filled, count(filled(d, S_XP + n, True)))
                    act.wait_ge(y_added, count(d.back * UM))
                    nc.scalar.activation(xp[:, n], mix_ps[:], ACT.Identity,
                                         bias=b_pin[:, n:n + 1]).then_inc(mix_drained, 1)
                elif name == "s_delta":
                    ssm_delta(d)
                elif name == "s_plus":
                    act.wait_ge(s_delta, count(d.ssm + 1))
                    act.wait_ge(bx_done, count(units(d)))
                    act.dma_start(dl_dram, sp_d).then_inc(dl_stored, 16)
                elif name == "c_y" and n == 0:
                    act.wait_ge(reduced, count((d.ssm + 1) * PS))
                    nc.scalar.copy(h_sum, mix_ps[0:NST, :]).then_inc(mix_drained, 1)
                elif name == "s_out":
                    act.wait_ge(mix_filled, count(filled(d, S_PO + n, True)))
                    nc.scalar.activation(pre[:, n], mix_ps[:], ACT.Identity,
                                         bias=b_pout[:, n:n + 1]).then_inc(mix_drained, 1)
                elif name == "s_mean":
                    square(drained(d, S_MEAN + 1))
                elif name == "s_var":
                    inv_std(filled(d, S_VAR, True), drained(d, S_VAR + 1))

            def gate_tanh(layer, d, t):
                act.wait_ge(gu_filled, count(ffn_count(d, 1) + t + 1))
                act.wait_ge(gu_drained, count(ffn_count(d, 1) + t - 1))
                nc.scalar.activation(tanh_g[:, t % 2], gate_ps[t % 2][:], ACT.Tanh,
                                     scale=0.5).then_inc(tanh_g_done, 1)

            def norm_square(n):
                act.wait_ge(norm_drained, count(2 * n - 1))
                nc.scalar.activation(sq_f[:], pre_f[:], ACT.Square).then_inc(squared_f, 1)

            def norm_inv_std(n):
                act.wait_ge(norm_filled, count(2 * n))
                nc.scalar.activation(rstd_f[:], out_ps[1][:], ACT.Ln, bias=eps_b[:]).then_inc(norm_drained, 1)
                act.wait_ge(norm_drained, count(2 * n))
                nc.scalar.activation(rstd_f[:], rstd_f[:], ACT.Exp, scale=-0.5).then_inc(rstd_f_done, 1)

            def head(layer, d, former):
                e = E1 if layer else E0
                act.wait_ge(x_ready[2 * layer], count((d.f1 if layer else d.f0) + 1))
                act.wait_ge(gu_filled, count(ffn_count(d, 1)))
                nc.scalar.activation(x_parts[:, 0], xs[2 * layer][:], ACT.Copy).then_inc(x_high, 1)
                act.wait_ge(shifted, count(d.f0 + d.f1 + 1))
                if layer == 0:
                    nc.scalar.activation(prob[:, :, E0:], logits[:, :, E0:], ACT.Tanh, scale=0.5)
                nc.scalar.activation(prob[:, :, 0:e], coef[:, :, 0:e], ACT.Exp).then_inc(prob_done, 1)
                if former:
                    norm_square(d.f0 + d.f1)
                gate_tanh(layer, d, 0)
                if former:
                    norm_inv_std(d.f0 + d.f1)

            def tile(layer, d, t):
                if t + 1 < TILES[layer]:
                    gate_tanh(layer, d, t + 1)

            def norm(layer, d):
                norm_square(d.f0 + d.f1 + 1)
                norm_inv_std(d.f0 + d.f1 + 1)

            schedule(act, piece, head, tile, norm, steps)

        @block.vector
        def _(dve):
            steps = Steps(DVE_STEPS)

            def link(ins):
                ins.then_inc(dve_step, 1)
                dve.wait_ge(dve_step, count(steps.next()))

            dve.wait_ge(par_loaded, 32)
            nc.vector.tensor_scalar_mul(half_cw[:], conv_w, 0.5)
            nc.vector.tensor_scalar_mul(half_cb[:], conv_b, 0.5)
            dve.wait_ge(prep_act, 2)
            nc.vector.tensor_scalar_add(decay[:], decay[:], 1.0).then_inc(prep_dve, 1)
            dve.wait_ge(prep_dve, 1)
            nc.vector.reciprocal(decay[:], decay[:]).then_inc(prep_dve, 1)
            dve.wait_ge(prep_dve, 2)
            nc.vector.tensor_scalar_mul(neg_a[:], neg_a[:], -1.0).then_inc(prep_dve, 1)
            dve.wait_ge(prep_dve, 3)
            dve.wait_ge(prep_pool, 1)

            def on_blocks(a):
                return a.rearrange("p (a l) -> p a l", a=1).to_broadcast([P, KD, L])

            def flat(a):
                return a.rearrange("p a l -> p (a l)")

            def convolve(d, m):
                mix_drained_n, silu_done_n = counts(dve, drained(d, F_X + m + 1), d.front * 2 * CB + m - 1)
                dve.wait_ge(mix_drained, mix_drained_n)
                dve.wait_ge(silu_done, silu_done_n)
                h, x = half_x[:, m % 2], x_pad[:, m % 2]
                tap = nc.vector.tensor_scalar(h, x[:, CONV - 1:], half_cw[:, m, CONV - 1:], half_cb[:, m:m + 1],
                                              ALU.mult, ALU.add)
                for k in range(CONV - 2, -1, -1):
                    link(tap)
                    tap = nc.vector.scalar_tensor_tensor(h, x[:, k:k + L], half_cw[:, m, k:k + 1], h,
                                                         ALU.mult, ALU.add)
                tap.then_inc(conv_done, 1)

            def conv_silu(d, m):
                conv_done_n, tanh_done_n, bx_done_n = counts(
                    dve, d.front * CB + m + 1, d.front * 2 * CB + m + 1, units(d))
                dve.wait_ge(conv_done, conv_done_n)
                dve.wait_ge(tanh_done, tanh_done_n)
                dve.wait_ge(bx_done, bx_done_n)
                nc.vector.scalar_tensor_tensor(xu[:, m], tanh_m[:, m % 2], 1.0, half_x[:, m % 2],
                                               ALU.add, ALU.mult).then_inc(silu_done, 1)

            def delta_and_u(d):
                dve.wait_ge(softplus_log, count(d.front + 1))
                nc.vector.scalar_tensor_tensor(flat(delta[:]), flat(delta[:]), 0.0, flat(y[:]),
                                               ALU.max, ALU.add).then_inc(delta_done, 1)
                delta_done_n, mix_filled_n = counts(dve, d.front + 1, filled(d, F_XP))
                dve.wait_ge(delta_done, delta_done_n)
                dve.wait_ge(mix_filled, mix_filled_n)
                for m in range(CB):
                    last = nc.vector.tensor_scalar(y[:, m], xu[:, m], d_m[:, m:m + 1], None, ALU.mult)
                link(last)
                nc.vector.tensor_tensor(xu[:], xu[:], delta[:], ALU.mult).then_inc(u_done, 1)

            def z_silu(d, m):
                tanh_done_n, mix_drained_n = counts(dve, d.front * 2 * CB + CB + m + 1, drained(d, F_Z + m + 1))
                dve.wait_ge(tanh_done, tanh_done_n)
                dve.wait_ge(mix_drained, mix_drained_n)
                nc.vector.scalar_tensor_tensor(z_act[:, m], tanh_m[:, m % 2], 1.0, z_act[:, m],
                                               ALU.add, ALU.mult).then_inc(silu_done, 1)

            def scan(d, u):
                bx_done_n, da_done_n = counts(dve, units(d, u + 1), d.back * UM + u + 1)
                dve.wait_ge(bx_done, bx_done_n)
                dve.wait_ge(da_done, da_done_n)
                h = flat(h_buf[:, u % H_RING])
                nc.vector.tensor_tensor_scan(h, flat(d_a[:, u % DA_RING]), h, 0.0,
                                             ALU.mult, ALU.add).then_inc(scanned, 1)

            def add_y(d, u):
                g, c = mixer_unit(u)
                h = h_buf[:, u % H_RING]
                if on_dve(u):
                    scanned_n, c_loaded_n = counts(
                        dve, units(d, u + 1), 16 * (d.back * (GROUPS // BC_RING) + g // BC_RING + 1))
                    dve.wait_ge(scanned, scanned_n)
                    dve.wait_ge(c_loaded[g % BC_RING], c_loaded_n)
                    nc.vector.tensor_tensor(h, h, c_bc[:, g % BC_RING], ALU.mult).then_inc(dve_step, 1)
                    product, former = counts(dve, steps.next(), d.back * UM + u)
                    dve.wait_ge(dve_step, product)
                else:
                    product, former = counts(dve, pool_c(d, u), d.back * UM + u)
                    dve.wait_ge(hc_done, product)
                dve.wait_ge(y_added, former)
                for j in range(NS):
                    last = nc.vector.tensor_tensor(y[:, c], y[:, c], h[:, j], ALU.add)
                    if j < NS - 1:
                        link(last)
                last.then_inc(y_added, 1)

            def gate_y(d):
                y_added_n, silu_done_n = counts(dve, (d.back + 1) * UM, (d.back + 1) * 2 * CB)
                dve.wait_ge(y_added, y_added_n)
                dve.wait_ge(silu_done, silu_done_n)
                nc.vector.tensor_tensor(y[:], y[:], z_act[:], ALU.mult).then_inc(y_gated, 1)

            def residual(d, m):
                dve.wait_ge(mix_filled, count(filled(d, B_OUT + m)))
                nc.vector.tensor_tensor(pre[:, m], mix_ps[:], x_in[:, m], ALU.add).then_inc(mix_drained, 1)

            def center(mean_filled, signal, n):
                mix_filled_n, signal_n = counts(dve, mean_filled, n)
                dve.wait_ge(mix_filled, mix_filled_n)
                dve.wait_ge(signal, signal_n)
                nc.vector.tensor_tensor(pre, pre, on_blocks(mix_ps[:]), ALU.subtract).then_inc(mix_drained, 1)

            def scale(d, dst, ready):
                rstd_done_n, out_drained_n = counts(dve, d.back + d.ssm + 1, d.f0 + d.f1)
                dve.wait_ge(rstd_done, rstd_done_n)
                dve.wait_ge(out_drained, out_drained_n)
                nc.vector.tensor_tensor(dst[:], pre, on_blocks(rstd), ALU.mult).then_inc(ready, 1)

            def ssm_scan(d, u):
                h, g, c = h_buf[:, u % H_RING], u // KD, u % KD
                dve.wait_ge(bx_done, count(units(d, u + 1)))
                for j in range(NS):
                    s = g * NS + j
                    last = nc.vector.tensor_tensor_scan(h[:, j], decay[:, c, s:s + 1].to_broadcast([P, L]),
                                                        h[:, j], 0.0, ALU.mult, ALU.add)
                last.then_inc(scanned, 1)
                if c == KD - 1:
                    dve.wait_ge(scanned, count(units(d, u + 1)))
                    nc.vector.tensor_tensor(h, h, h_buf[:, (u - 1) % H_RING], ALU.add).then_inc(paired, 1)

            def piece(d, name, n):
                if name == "split" and n < SPLITS:
                    dve.wait_ge(w_high, n + 1)
                    half = 2 * (n % 2)
                    high = gu_ring[:, half:half + 2, 0:1].bitcast(F32)
                    nc.vector.tensor_tensor(gu_ring[:, half:half + 2, 1:2], raw[n % 2], high,
                                            ALU.subtract).then_inc(w_low, 1)
                elif name == "in":
                    if n < CB:
                        convolve(d, n)
                    if n >= 1:
                        conv_silu(d, n - 1)
                elif name == "u_y":
                    delta_and_u(d)
                elif name == "z" and n >= 1:
                    z_silu(d, n - 1)
                elif name == "unit":
                    if n >= Y_LAG:
                        add_y(d, n - Y_LAG)
                    if n < UM:
                        scan(d, n)
                elif name == "out":
                    if n == 0:
                        gate_y(d)
                    else:
                        residual(d, n - 1)
                elif name == "b_mean":
                    center(filled(d, B_MEAN), mix_drained, drained(d, B_OUT + KD))
                elif name == "b_norm":
                    scale(d, xs[0], x_ready[0])
                elif name == "s_plus":
                    dve.wait_ge(s_log, count(d.ssm + 1))
                    nc.vector.scalar_tensor_tensor(sp_d, sp_v, 0.0, sp_a, ALU.max, ALU.add).then_inc(s_delta, 1)
                elif name == "s_unit" and 1 <= n <= US:
                    ssm_scan(d, n - 1)
                elif name == "c_y":
                    dve.wait_ge(mix_filled, count(filled(d, S_YC + n, True)))
                    nc.vector.scalar_tensor_tensor(ys[:, n], xp[:, n], d_s[:, n:n + 1], mix_ps[:],
                                                   ALU.mult, ALU.add).then_inc(mix_drained, 1)
                elif name == "s_mean":
                    dve.wait_ge(mix_drained, count(drained(d, S_PO + KD)))
                    nc.vector.scalar_tensor_tensor(flat(pre), flat(xs[1][:]), 2.0, flat(pre),
                                                   ALU.mult, ALU.add).then_inc(ssm_pre, 1)
                    center(filled(d, S_MEAN, True), ssm_pre, d.ssm + 1)
                elif name == "s_norm":
                    scale(d, xs[2], x_ready[2])

            def router(layer, d):
                n = d.f0 + d.f1
                e, k = (E1, K1) if layer else (E0, K0)
                width = e if layer else e + 1
                dve.wait_ge(side_filled, count(side_count(d) + 1))
                nc.vector.tensor_copy(logits[:, :, 0:width], side_ps[:, 0:TT * width].rearrange(
                    "p (t e) -> p t e", t=TT)).then_inc(side_drained, 1)
                dve.wait_ge(side_drained, count(side_count(d) + 1))
                lg = logits[:, :, 0:e]
                link(nc.vector.tensor_reduce(top[:], lg, AX.X, ALU.max))
                nc.vector.tensor_tensor(coef[:, :, 0:e], lg, top[:].rearrange("p (t a) -> p t a", a=1).to_broadcast(
                    [P, TT, e]), ALU.subtract).then_inc(shifted, 1)
                gt, eq = (flat(a[:])[:, 0:TT * e * e].rearrange("p (t i j) -> p t i j", t=TT, i=e)
                          for a in (greater, equal))
                lj = lg.unsqueeze(2).to_broadcast([P, TT, e, e])
                li = lg.unsqueeze(3).to_broadcast([P, TT, e, e])
                lower = before[:, 0:e, 0:e].unsqueeze(1).to_broadcast([P, TT, e, e])
                nc.vector.tensor_tensor(gt, lj, li, ALU.is_gt)
                link(nc.vector.tensor_tensor(eq, lj, li, ALU.is_equal))
                link(nc.vector.tensor_tensor(eq, eq, lower, ALU.mult))
                link(nc.vector.tensor_tensor(gt, gt, eq, ALU.add))
                rk = rank[:, :, 0:e]
                nc.vector.tensor_reduce(rk, gt, AX.X, ALU.add).then_inc(dve_step, 1)
                dve_step_n, prob_done_n = counts(dve, steps.next(), n + 1)
                dve.wait_ge(dve_step, dve_step_n)
                dve.wait_ge(prob_done, prob_done_n)
                pr, cf = prob[:, :, 0:e], coef[:, :, 0:e]
                if layer == 0:
                    nc.vector.tensor_scalar(coef[:, :, E0:], prob[:, :, E0:], 0.25, 0.25, ALU.mult, ALU.add)
                link(nc.vector.scalar_tensor_tensor(cf, rk, float(k), pr, ALU.is_lt, ALU.mult))
                link(nc.vector.tensor_reduce(top[:], cf if layer else pr, AX.X, ALU.add))
                link(nc.vector.reciprocal(inv[:], top[:]))
                nc.vector.scalar_tensor_tensor(
                    cf, cf, 0.5, inv[:].rearrange("p (t a) -> p t a", a=1).to_broadcast([P, TT, e]),
                    ALU.mult, ALU.mult).then_inc(coef_done, 1)

            def split_coef(layer, d):
                width = E1 if layer else E0 + 1
                dve.wait_ge(side_filled, count(side_count(d) + 2))
                hi, ct = coef_parts[0:width, :], side_ps[0:width, :]
                r, md = rest[0:width, :], mid[0:width, :]
                link(nc.vector.tensor_copy(hi, ct))
                link(nc.vector.tensor_tensor(r, ct, hi, ALU.subtract))
                link(nc.vector.tensor_copy(md, r))
                nc.vector.tensor_copy(coef_parts[EPART:EPART + width, :], md)
                nc.vector.tensor_tensor(coef_parts[2 * EPART:2 * EPART + width, :], r, md,
                                        ALU.subtract).then_inc(side_drained, 1)

            def gate_up(layer, d, t):
                dve.wait_ge(tanh_g_done, count(ffn_count(d, 1) + t + 1))
                silu2 = tanh_g[:, t % 2]
                nc.vector.scalar_tensor_tensor(silu2, silu2, 1.0, gate_ps[t % 2][:],
                                               ALU.add, ALU.mult).then_inc(dve_step, 1)
                dve_step_n, side_drained_n = counts(dve, steps.next(), side_count(d) + 2 + max(t - 1, 0))
                dve.wait_ge(dve_step, dve_step_n)
                dve.wait_ge(side_drained, side_drained_n)
                nc.vector.tensor_tensor(gated_u[:, t % 2], up_ps[t % 2][:], silu2, ALU.mult).then_inc(
                    gu_drained, 1)

            def weight_hidden(layer, d, t):
                side_filled_n, gu_drained_n, tile_done_n = counts(
                    dve, side_count(d) + 3 + t, ffn_count(d, 1) + t + 1, ffn_count(d, 1) + t - 1)
                dve.wait_ge(side_filled, side_filled_n)
                dve.wait_ge(gu_drained, gu_drained_n)
                dve.wait_ge(tile_done, tile_done_n)
                nc.vector.tensor_tensor(hid[:, t % 2], side_ps[:], gated_u[:, t % 2], ALU.mult).then_inc(
                    side_drained, 1)

            def ffn_residual(layer, d):
                tile_done_n, out_stored_n = counts(dve, ffn_count(d, 1) + TILES[layer], 16 * (d.f1 + 1))
                dve.wait_ge(tile_done, tile_done_n)
                dve.wait_ge(out_stored, out_stored_n)
                for m in range(KD):
                    last = nc.vector.tensor_tensor(pre_f[:, m], out_ps[m][:], xs[2 * layer][:, m], ALU.add)
                last.then_inc(out_drained, 1)

            def norm_center(n):
                norm_filled_n, out_drained_n = counts(dve, 2 * n - 1, n)
                dve.wait_ge(norm_filled, norm_filled_n)
                dve.wait_ge(out_drained, out_drained_n)
                nc.vector.tensor_tensor(pre_f[:], pre_f[:], on_blocks(out_ps[0][:]),
                                        ALU.subtract).then_inc(norm_drained, 1)

            def norm_scale(layer, n, ssms):
                rstd_f_done_n, ssm_pre_n = counts(dve, n, ssms)
                dve.wait_ge(rstd_f_done, rstd_f_done_n)
                dve.wait_ge(ssm_pre, ssm_pre_n)
                dst, ready = (pre_f, out_ready) if layer else (xs[1], x_ready[1])
                nc.vector.tensor_tensor(dst[:], pre_f[:], on_blocks(rstd_f[:]), ALU.mult).then_inc(ready, 1)

            def head(layer, d, former):
                if former:
                    ffn_residual(*former)
                dve.wait_ge(x_high, count(d.f0 + d.f1 + 1))
                nc.vector.tensor_tensor(x_parts[:, 1], xs[2 * layer][:], x_parts[:, 0].bitcast(F32),
                                        ALU.subtract).then_inc(x_low, 1)
                router(layer, d)
                if former:
                    norm_center(d.f0 + d.f1)
                split_coef(layer, d)
                gate_up(layer, d, 0)
                if former:
                    norm_scale(former[0], d.f0 + d.f1, d.ssm)

            def tile(layer, d, t):
                weight_hidden(layer, d, t)
                if t + 1 < TILES[layer]:
                    gate_up(layer, d, t + 1)

            def norm(layer, d):
                n = d.f0 + d.f1 + 1
                ffn_residual(layer, d)
                norm_center(n)
                norm_scale(layer, n, 0)

            schedule(dve, piece, head, tile, norm, steps)

        @block.tensor
        def _(pe):
            pe.wait_ge(par_loaded, 32)
            pe.wait_ge(prep_pool, 1)

            def project(w, lo, src, blocks, rows=P):
                for k in range(blocks):
                    last = nc.tensor.matmul(mix_ps[0:rows, :], w[:, k, lo:lo + rows], src[:, k],
                                            start=(k == 0), stop=(k == blocks - 1))
                return last

            def mean(src, bank):
                for k in range(KD):
                    last = nc.tensor.matmul(bank[:], mean_w[:], src[:, k], start=(k == 0), stop=(k == KD - 1))
                return last

            def reduce_pair(d, p):
                pe.wait_ge(paired, count(d.ssm * PS + p + 1))
                for j in range(NS):
                    s = p * NS + j
                    last = nc.tensor.matmul(mix_ps[0:NST, :], onecol[:, NST - 1 - s:2 * NST - 1 - s],
                                            h_buf[:, (KD * p + KD - 1) % H_RING, j], start=(s == 0),
                                            stop=(s == NST - 1))
                last.then_inc(reduced, 1)

            def piece(d, name, n):
                if name == "in" and n < CB:
                    pe.wait_ge(mix_drained, count(drained(d, F_X + n)))
                    pe.wait_ge(x_loaded, count(16 * (d.front + 1)))
                    project(w_in, n * P, x_in, KD).then_inc(mix_filled, 1)
                elif name == "x_proj":
                    pe.wait_ge(mix_drained, count(drained(d, F_XP)))
                    pe.wait_ge(silu_done, count(d.front * 2 * CB + CB))
                    project(w_x, 0, xu, CB, XD).then_inc(mix_filled, 1)
                elif name == "dt":
                    pe.wait_ge(mix_drained, count(drained(d, F_DT + n)))
                    nc.tensor.matmul(mix_ps[:], w_dt[0:RANK, n * P:(n + 1) * P], x_dbl[0:RANK, :],
                                     start=True, stop=True).then_inc(mix_filled, 1)
                elif name == "z" and n < CB:
                    pe.wait_ge(mix_drained, count(drained(d, F_Z + n)))
                    project(w_in, DI + n * P, x_in, KD).then_inc(mix_filled, 1)
                elif name == "out" and n < KD:
                    pe.wait_ge(mix_drained, count(drained(d, B_OUT + n)))
                    pe.wait_ge(y_gated, count(d.back + 1))
                    project(w_out, n * P, y, CB).then_inc(mix_filled, 1)
                elif name == "b_mean":
                    pe.wait_ge(mix_drained, count(drained(d, B_MEAN)))
                    mean(pre, mix_ps).then_inc(mix_filled, 1)
                elif name == "b_var":
                    pe.wait_ge(mix_drained, count(drained(d, B_VAR)))
                    pe.wait_ge(squared, count(d.back + d.ssm + 1))
                    mean(sq, mix_ps).then_inc(mix_filled, 1)
                elif name == "xp":
                    pe.wait_ge(mix_drained, count(drained(d, S_XP + n)))
                    pe.wait_ge(x_ready[1], count(d.ssm + 1))
                    project(w_pin, n * P, xs[1], KD).then_inc(mix_filled, 1)
                elif name == "s_delta":
                    pe.wait_ge(mix_drained, count(drained(d, S_DL)))
                    project(w_b, 0, xp, KD, NST).then_inc(mix_filled, 1)
                elif name == "s_unit" and n >= KD + 1 and n % KD == 1:
                    if n == KD + 1:
                        pe.wait_ge(mix_drained, count(drained(d, S_H)))
                    reduce_pair(d, n // KD - 1)
                elif name == "c_y":
                    pe.wait_ge(mix_drained, count(drained(d, S_YC + n)))
                    nc.tensor.matmul(mix_ps[:], c_w[0:NST, n * P:(n + 1) * P], h_sum,
                                     start=True, stop=True).then_inc(mix_filled, 1)
                elif name == "s_out":
                    pe.wait_ge(mix_drained, count(drained(d, S_PO + n)))
                    project(w_pout, n * P, ys, KD).then_inc(mix_filled, 1)
                elif name == "s_mean":
                    pe.wait_ge(mix_drained, count(drained(d, S_MEAN)))
                    pe.wait_ge(ssm_pre, count(d.ssm + 1))
                    mean(pre, mix_ps).then_inc(mix_filled, 1)
                elif name == "s_var":
                    pe.wait_ge(mix_drained, count(drained(d, S_VAR)))
                    pe.wait_ge(squared, count(d.back + d.ssm + 1))
                    mean(sq, mix_ps).then_inc(mix_filled, 1)

            def gate_and_up(layer, d, t):
                slots = d.f0 * (T0 // W_RING) + d.f1 * (T1 // W_RING) + t // W_RING + 1
                pe.wait_ge(w_loaded[t % W_RING], count(32 * slots))
                pe.wait_ge(gu_drained, count(ffn_count(d, 1) + t - 1))
                if t == 0:
                    pe.wait_ge(x_low, count(d.f0 + d.f1 + 1))
                high, low = gu_ring[:, t % W_RING, 0], gu_ring[:, t % W_RING, 1]
                for which, bank in ((0, gate_ps[t % 2]), (1, up_ps[t % 2])):
                    for k in range(KD):
                        lo = (which * KD + k) * P
                        for w, part in ((high, 0), (high, 1), (low, 0)):
                            last = nc.tensor.matmul(bank[:], w[:, lo:lo + P], x_parts[:, part, k],
                                                    start=(k == 0 and w is high and part == 0),
                                                    stop=(k == KD - 1 and w is low))
                last.then_inc(gu_filled, 1)

            def down(layer, d, t):
                pe.wait_ge(side_drained, count(side_count(d) + 3 + t))
                if t == 0:
                    pe.wait_ge(norm_drained, count(2 * (d.f0 + d.f1)))
                w = down_ring[:, t % W_RING]
                for m in range(KD):
                    last = nc.tensor.matmul(out_ps[m][:], w[:, m * P:(m + 1) * P], hid[:, t % 2],
                                            start=(t == 0), stop=(t == TILES[layer] - 1))
                last.then_inc(tile_done, 1)

            def spread_coef(layer, d, t):
                pe.wait_ge(side_drained, count(side_count(d) + 2 + t))
                which = T0 + t // (I1 // P) if layer else t
                nc.tensor.matmul(side_ps[:], sel_sb[:, which], coef_parts[:], start=True,
                                 stop=True).then_inc(side_filled, 1)

            def norm_mean(n):
                pe.wait_ge(out_drained, count(n))
                mean(pre_f, out_ps[0]).then_inc(norm_filled, 1)

            def norm_var(n):
                pe.wait_ge(squared_f, count(n))
                mean(sq_f, out_ps[1]).then_inc(norm_filled, 1)

            def head(layer, d, former):
                x, width = xs[2 * layer], E1 if layer else E0 + 1
                pe.wait_ge(x_ready[2 * layer], count((d.f1 if layer else d.f0) + 1))
                pe.wait_ge(side_drained, count(side_count(d)))
                for tt in range(TT):
                    for k in range(KD):
                        last = nc.tensor.matmul(side_ps[:, tt * width:(tt + 1) * width],
                                                x[:, k, tt * P:(tt + 1) * P], gates[layer][:, k],
                                                start=(k == 0), stop=(k == KD - 1))
                last.then_inc(side_filled, 1)
                gate_and_up(layer, d, 0)
                if former:
                    norm_mean(d.f0 + d.f1)
                pe.wait_ge(coef_done, count(d.f0 + d.f1 + 1))
                pe.wait_ge(side_drained, count(side_count(d) + 1))
                for tt in range(TT):
                    last = nc.tensor.matmul(side_ps[0:width, tt * P:(tt + 1) * P], coef[:, tt, 0:width], ident,
                                            start=True, stop=True)
                last.then_inc(side_filled, 1)
                gate_and_up(layer, d, 1)
                if former:
                    norm_var(d.f0 + d.f1)
                spread_coef(layer, d, 0)

            def tile(layer, d, t):
                if t + 2 < TILES[layer]:
                    gate_and_up(layer, d, t + 2)
                down(layer, d, t)
                if t + 1 < TILES[layer]:
                    spread_coef(layer, d, t + 1)

            def norm(layer, d):
                norm_mean(d.f0 + d.f1 + 1)
                norm_var(d.f0 + d.f1 + 1)

            schedule(pe, piece, head, tile, norm)


ACT_STEPS = 4
DVE_STEPS = 135


def kernel(**inputs):
    import concourse.bacc as bacc
    from concourse.bass_utils import run_bass_kernel_spmd

    a = {k: np.asarray(v) for k, v in inputs.items()}

    def rows(w, blocks):
        n = w.shape[0] // blocks
        return np.ascontiguousarray(w.reshape(blocks, n, -1).transpose(1, 0, 2)).reshape(n, -1)

    def padded(w):
        full = np.zeros((P, w.shape[1]), w.dtype)
        full[:w.shape[0]] = w
        return full

    onecol = np.zeros((P, 2 * NST - 1), np.float32)
    onecol[:, NST - 1] = 1.0
    before = np.broadcast_to(np.tril(np.ones((E0, E0), np.float32), -1).reshape(1, -1), (P, E0 * E0))
    gate0 = np.concatenate([a["L0_ffn_gate_w"], a["L0_ffn_sgate_w"]], 0).T
    values = {
        "w_in": rows(a["L0_attn_in_proj_w"].T, KD), "w_x": rows(a["L0_attn_x_proj_w"].T, CB),
        "w_out": rows(a["L0_attn_out_proj_w"].T, CB), "w_dt": padded(a["L0_attn_dt_proj_w"].T),
        "c_w": padded(a["L1_attn_C_w"].T), "w_pin": rows(a["L1_attn_proj_in_w"].T, KD),
        "w_pout": rows(a["L1_attn_proj_out_w"].T, KD), "w_b": rows(a["L1_attn_B_w"].T, KD),
        "gate0": rows(gate0, KD), "gate1": rows(a["L1_ffn_gate_kernel"], KD),
        "ident": np.eye(P, dtype=np.float32), "onecol": onecol, "conv_w": rows(a["L0_attn_conv_w"], CB),
        "conv_b": rows(a["L0_attn_conv_b"][:, None], CB), "dt_b": rows(a["L0_attn_dt_proj_b"][:, None], CB),
        "a_log": rows(a["L0_attn_A_log"], CB), "d_m": rows(a["L0_attn_D"][:, None], CB),
        "b_pin": rows(a["L1_attn_proj_in_b"][:, None], KD), "b_pout": rows(a["L1_attn_proj_out_b"][:, None], KD),
        "a_s": rows(a["L1_attn_A"], KD), "d_s": rows(a["L1_attn_D_param"][:, None], KD), "before": before,
    }
    params = np.concatenate([values[name] for name, _ in PARAMS], 1)

    def hidden_tiles(gate, up, dn, tiles):
        pad = tiles * P - gate.shape[1]
        g, u = (np.pad(w, ((0, 0), (0, pad))).reshape(KD, P, tiles, P).transpose(2, 1, 0, 3).reshape(
            tiles, P, KD * P) for w in (gate, up))
        return np.concatenate([g, u], 2), np.pad(dn, ((0, pad), (0, 0))).reshape(tiles, P, D)

    w13, w2 = a["L0_ffn_w13"], a["L0_ffn_w2"]
    sgu, sdn = a["L0_ffn_shared_gate_up_w"], a["L0_ffn_shared_down_w"]
    ffn0 = hidden_tiles(np.concatenate([w13[:, :I0].reshape(-1, D), sgu[:IS]], 0).T,
                        np.concatenate([w13[:, I0:].reshape(-1, D), sgu[IS:]], 0).T,
                        np.concatenate([w2.transpose(0, 2, 1).reshape(-1, D), sdn.T], 0), T0)
    ffn1 = hidden_tiles(a["L1_ffn_w0_kernel"].transpose(1, 0, 2).reshape(D, -1),
                        a["L1_ffn_w1_kernel"].transpose(1, 0, 2).reshape(D, -1),
                        a["L1_ffn_wo_kernel"].reshape(-1, D), T1)
    gu_w, down_w = (np.ascontiguousarray(np.concatenate(w, 0)) for w in zip(ffn0, ffn1))

    sel = np.zeros((3 * EPART, T0 + E1, P), np.float32)
    for t in range(T0):
        for i in range(P):
            unit = t * P + i
            expert = unit // I0 if unit < E0 * I0 else E0
            sel[[expert, EPART + expert, 2 * EPART + expert], t, i] = 1.0
    for e in range(E1):
        sel[[e, EPART + e, 2 * EPART + e], T0 + e, :] = 1.0
    sel = sel.astype(mybir.dt.np(BF16))

    xT = np.ascontiguousarray(a["L0_attn_hidden_states"].reshape(BATCH * L, D).T)
    nc = bacc.Bacc("TRN2", target_bir_lowering=False, num_devices=1)
    x_d = nc.dram_tensor("xT", [D, BATCH * L], F32, kind="ExternalInput").ap()
    p_d = nc.dram_tensor("params", [P, NPAR], F32, kind="ExternalInput").ap()
    s_d = nc.dram_tensor("sel", list(sel.shape), BF16, kind="ExternalInput").ap()
    g_d = nc.dram_tensor("gu_w", list(gu_w.shape), F32, kind="ExternalInput").ap()
    w_d = nc.dram_tensor("down_w", list(down_w.shape), F32, kind="ExternalInput").ap()
    o_d = nc.dram_tensor("outT", [D, BATCH * L], F32, kind="ExternalOutput").ap()
    build(nc, x_d.rearrange("(k p) n -> p k n", p=P), p_d, s_d, g_d, w_d, o_d.rearrange("(k p) n -> p k n", p=P))
    res = run_bass_kernel_spmd(nc, [{"xT": xT, "params": params, "sel": sel, "gu_w": gu_w, "down_w": down_w}], core_ids=[0])
    return np.ascontiguousarray(res.results[0]["outT"].T).reshape(BATCH, L, D)
```

```python
from collections import namedtuple
from contextlib import ExitStack

import numpy as np

import concourse.bass as bass
from concourse import mybir

F32 = mybir.dt.float32
F32R = mybir.dt.float32r
BF16 = mybir.dt.bfloat16
ALU = mybir.AluOpType
ACT = mybir.ActivationFunctionType
AX = mybir.AxisListType

P = 128
BATCH, L, D = 8, 512, 256
KD = D // P
DI, CONV, NST, RANK = 512, 4, 16, 16
CB = DI // P
XD = RANK + 2 * NST
E0, K0, I0, IS = 16, 4, 176, 704
E1, K1, I1 = 8, 2, 512
T0 = -(-(E0 * I0 + IS) // P)
T1 = E1 * I1 // P
TILES = (T0, T1)
GU = 2 * D
SPLITS = (T0 + T1) // 2
SPLIT_OVER = 45
EPS = 1e-5

NS = 2
GROUPS = NST // NS
UM = GROUPS * CB
US = GROUPS * KD
PS = US // KD
BC_RING, DA_RING, H_RING, W_RING = 4, 2, 4, 4
EPART = 32

PARAMS = [("w_in", KD * 2 * DI), ("w_x", CB * XD), ("w_out", CB * D), ("w_dt", DI), ("c_w", D),
          ("w_pin", KD * D), ("w_pout", KD * D), ("w_b", KD * NST), ("gate0", KD * (E0 + 1)),
          ("gate1", KD * E1), ("ident", P), ("onecol", 2 * NST - 1), ("conv_w", CB * CONV),
          ("conv_b", CB), ("dt_b", CB), ("a_log", CB * NST), ("d_m", CB), ("b_pin", KD),
          ("b_pout", KD), ("a_s", KD * NST), ("d_s", KD), ("before", E0 * E0)]
OFF, NPAR = {}, 0
for _name, _n in PARAMS:
    OFF[_name] = (NPAR, NPAR + _n)
    NPAR += _n

F_X, F_XP, F_DT = 0, CB, CB + 1
F_Z = F_DT + CB
NF = F_Z + CB
B_OUT, B_MEAN, B_VAR, B_ROUTE, NB = 0, KD, KD + 1, KD + 2, KD + 3
S_XP, S_DL, S_H, S_YC, S_PO, S_MEAN, S_VAR = 0, KD, KD + 1, KD + 2, 2 * KD + 2, 3 * KD + 2, 3 * KD + 3
S_ROUTE, NSF = S_VAR + 1, S_VAR + 2
SSM_END, FRONT_END = 15, 22
EARLY = 6
TAIL = 3
STORE_TILE = 4
DOWN_AHEAD = 1
C_EXTRA = 1
Y_LAG = 2
ROWS = {("u_y", 0): "b0", ("u_y", 1): "b1", ("u_y", 2): "c0", ("unit", 0): "c1", ("unit", 1): "b2",
        ("unit", 2): "c2", ("unit", 3): "b3", ("unit", 4): "c3"}
ROWS_LAG = 3
for _g in range(BC_RING, GROUPS, 2):
    for _i, _rows in enumerate((f"b{_g}", f"b{_g + 1}", f"c{_g}", f"c{_g + 1}")):
        ROWS["unit", 2 * CB * (_g // 2 - BC_RING // 2 + 1) + Y_LAG - 1 + ROWS_LAG + _i] = _rows
FIRST_C, DVE_C = (2, 4), 8

Done = namedtuple("Done", "front back ssm f0 f1")


def mixer_unit(u):
    return 2 * (u // (2 * CB)) + u % 2, (u // 2) % CB


def ahead(n):
    return range(n + 1 if n else 0, min(n + 2, UM))


def dve_c(row):
    return FIRST_C[row] if isinstance(row, int) and row < len(FIRST_C) else DVE_C


def on_dve(row, u):
    return u % dve_c(row) == dve_c(row) - 1


FRONT = ([("in", m) for m in range(CB + 1)] + [("x_proj", 0)] + [("dt", m) for m in range(CB)]
         + [("softplus", 0), ("z", 0), ("softplus", 1), ("softplus", 2)] + [("u_y", i) for i in range(3)]
         + [("z", m) for m in range(1, CB + 1)])
BACK = [("unit", u) for u in range(UM + Y_LAG)] + [("out", m) for m in range(KD + 1)] + [
    ("b_mean", 0), ("b_var", 0), ("b_norm", 0)] + [("route0", i) for i in range(5)]
SSM = ([("xp", m) for m in range(KD)] + [("s_delta", 0), ("s_plus", 0)] + [("s_unit", u) for u in range(US + 2)]
       + [("c_y", m) for m in range(KD)] + [("s_out", m) for m in range(KD)]
       + [("s_mean", 0), ("s_var", 0), ("s_norm", 0)] + [("route1", i) for i in range(5)])


UP_TO_U = FRONT.index(("u_y", 2)) + 1

BACK_END, SSM_LAST = BACK.index(("b_norm", 0)), SSM.index(("s_norm", 0))
UP_TO_DELTA = SSM.index(("s_plus", 0)) + 1


def at(d, pieces):
    return [(d, name, n) for name, n in pieces]


def merge(few, many):
    every = len(many) // len(few)
    return [p for i, q in enumerate(many) for p in [q] + (few[i // every:i // every + 1] if i % every == 0 else [])]


def spread(tiles, *parts):
    plan = [[] for _ in range(tiles)]
    for pieces, lo, hi in parts:
        for i, p in enumerate(pieces):
            plan[lo + i * (hi - lo) // len(pieces)].append(p)
    return plan


class Steps:

    def __init__(self, per_row):
        self.per_row, self.base, self.n = per_row, 0, 0

    def loop(self, i):
        self.start, self.base, self.n = self.n, self.n + (i - 1) * self.per_row, 0

    def behind(self):
        assert self.n == self.per_row, self.n
        self.base, self.n = self.start + (BATCH - 3) * self.per_row, 0

    def next(self):
        self.n += 1
        return self.base + self.n


def build(nc, xT, params, sel, gu_w, down_w, out):
    with ExitStack() as ctx:
        def sb(name, shape, dt=F32):
            return ctx.enter_context(nc.sbuf_tensor(name, shape, dt))

        def ps(name, shape):
            return ctx.enter_context(nc.psum_tensor(name, shape, F32))

        def sem(name):
            return ctx.enter_context(nc.semaphore(name))

        par = sb("par", [P, NPAR])

        def cols(name, **dims):
            a, b = OFF[name]
            v = par[:, a:b]
            return v.rearrange("p (a b) -> p a b", **dims) if dims else v

        w_in, w_x, w_out = cols("w_in", a=KD), cols("w_x", a=CB), cols("w_out", a=CB)
        w_dt, c_w = cols("w_dt"), cols("c_w")
        w_pin, w_pout, w_b = cols("w_pin", a=KD), cols("w_pout", a=KD), cols("w_b", a=KD)
        gates = (cols("gate0", a=KD), cols("gate1", a=KD))
        ident, onecol, conv_w = cols("ident"), cols("onecol"), cols("conv_w", a=CB)
        conv_b, dt_b, a_log, d_m = cols("conv_b"), cols("dt_b"), cols("a_log", a=CB), cols("d_m")
        b_pin, b_pout, a_s, d_s = cols("b_pin"), cols("b_pout"), cols("a_s", a=KD), cols("d_s")
        before = cols("before", a=E0)
        sel_sb = sb("sel_sb", [3 * EPART, T0 + E1, P], BF16)
        mean_w = sb("mean_w", [P, P])
        eps_b = sb("eps_b", [P, 1])
        neg_a = sb("neg_a", [P, CB, NST])
        decay = sb("decay", [P, KD, NST])
        half_cw = sb("half_cw", [P, CB, CONV])
        half_cb = sb("half_cb", [P, CB])

        x_in = sb("x_in", [P, KD, L])
        x_pad = sb("x_pad", [P, 2, CONV - 1 + L])
        half_x = sb("half_x", [P, 2, L])
        tanh_m = sb("tanh_m", [P, 2, L])
        xu = sb("xu", [P, CB, L])
        delta = sb("delta", [P, CB, L])
        y = sb("y", [P, CB, L])
        z_act = sb("z_act", [P, CB, L])
        x_dbl = sb("x_dbl", [XD, L])
        b_bc = sb("b_bc", [P, BC_RING, NS, L])
        c_bc = sb("c_bc", [P, BC_RING, NS, L])
        d_a = sb("d_a", [P, DA_RING, NS, L])
        h_buf = sb("h_buf", [P, H_RING, NS, L])
        pre, sq, rstd = h_buf[:, 0], h_buf[:, 1], h_buf[:, 2, 0]
        assert NS == KD
        xp, ys = c_bc[:, 0], c_bc[:, 1]
        sp_v, sp_a, sp_d, h_sum = (c_bc[0:NST, 2 + i // NS, i % NS] for i in range(4))
        xs = [sb(f"x{i}", [P, KD, L]) for i in (1, 2, 3)]
        gu_ring = sb("gu_ring", [P, W_RING, 2, GU], F32R)
        down_ring = sb("down_ring", [P, W_RING, D])
        x_parts = sb("x_parts", [P, 2, KD, L], F32R)
        tanh_g = sb("tanh_g", [P, 2, L])
        gated_u = sb("gated_u", [P, 2, L])
        hid = sb("hid", [P, 2, L])
        pre_f = sb("pre_f", [P, KD, L])
        sq_f = sb("sq_f", [P, KD, L])
        rstd_f = sb("rstd_f", [P, L])
        coef_parts = sb("coef_parts", [3 * EPART, L], BF16)
        rest = sb("rest", [E0 + 1, L])
        mid = sb("mid", [E0 + 1, L], BF16)
        TT = L // P
        logits = sb("logits", [P, TT, E0 + 1])
        prob = sb("prob", [P, TT, E0 + 1])
        coef = sb("coef", [P, TT, E0 + 1])
        rank = sb("rank", [P, TT, E0])
        top = sb("top", [P, TT])
        inv = sb("inv", [P, TT])
        greater, equal = h_buf[:, 3], h_buf[:, 1]
        raw = [a[:].rearrange("p a (b l) -> p a b l", b=1) for a in (pre_f, sq_f)]

        gate_ps = [ps(f"gate_ps{i}", [P, L]) for i in range(2)]
        up_ps = [ps(f"up_ps{i}", [P, L]) for i in range(2)]
        side_ps = ps("side_ps", [P, L])
        out_ps = [ps(f"out_ps{i}", [P, L]) for i in range(KD)]
        mix_ps = ps("mix_ps", [P, L])

        bc_dram = nc.dram_tensor("bc_scratch", [2 * NST, L], F32, kind="Internal").ap()
        gu_dram = nc.dram_tensor("gu_split", [T0 + T1, P, 2, GU], F32, kind="Internal").ap()
        dl_dram = nc.dram_tensor("dl_scratch", [NST, L], F32, kind="Internal").ap()

        par_loaded = sem("par_loaded")
        prep_act = sem("prep_act")
        prep_dve = sem("prep_dve")
        prep_pool = sem("prep_pool")
        act_step, dve_step = sem("act_step"), sem("dve_step")
        raw_loaded = [sem(f"raw_loaded{i}") for i in range(2)]
        w_high, w_low = sem("w_high"), sem("w_low")
        split_stored = [sem(f"split_stored{i}") for i in range(2)]
        x_high, x_low = sem("x_high"), sem("x_low")
        x_loaded = sem("x_loaded")
        mix_filled, mix_drained = sem("mix_filled"), sem("mix_drained")
        conv_done, tanh_done, silu_done = sem("conv_done"), sem("tanh_done"), sem("silu_done")
        bc_stored, dl_stored = sem("bc_stored"), sem("dl_stored")
        b_loaded = [sem(f"b_loaded{i}") for i in range(BC_RING)]
        c_loaded = [sem(f"c_loaded{i}") for i in range(BC_RING)]
        softplus_log = sem("softplus_log")
        delta_done, u_done = sem("delta_done"), sem("u_done")
        da_done, bx_done, scanned = sem("da_done"), sem("bx_done"), sem("scanned")
        hc_done, y_added = sem("hc_done"), sem("y_added")
        paired, reduced = sem("paired"), sem("reduced")
        y_gated = sem("y_gated")
        squared, rstd_done = sem("squared"), sem("rstd_done")
        x_ready = [sem(f"x{i}_ready") for i in (1, 2, 3)]
        s_log, s_delta, ssm_pre = sem("s_log"), sem("s_delta"), sem("ssm_pre")
        gu_loaded = [sem(f"gu_loaded{i}") for i in range(W_RING)]
        down_loaded = [sem(f"down_loaded{i}") for i in range(W_RING)]
        side_filled, side_drained = sem("side_filled"), sem("side_drained")
        shifted, prob_done, coef_done = sem("shifted"), sem("prob_done"), sem("coef_done")
        gu_filled, tanh_g_done, gu_drained = sem("gu_filled"), sem("tanh_g_done"), sem("gu_drained")
        tile_done = sem("tile_done")
        out_drained = sem("out_drained")
        norm_filled, norm_drained = sem("norm_filled"), sem("norm_drained")
        squared_f, rstd_f_done = sem("squared_f"), sem("rstd_f_done")
        out_ready, out_stored = sem("out_ready"), sem("out_stored")

        def ffn_count(d, per_tile, extra=0):
            return d.f0 * (T0 * per_tile + extra) + d.f1 * (T1 * per_tile + extra)

        def side_count(d):
            return ffn_count(d, 1, C_EXTRA)

        def drained(d, j=0):
            return d.front * NF + d.back * NB + d.ssm * NSF + j

        def filled(d, j, ssm=False):
            return d.front * NF + d.back * NB + d.ssm * (NSF - 1) + (j if ssm and j >= S_H else j + 1)

        def units(d, u=0):
            return d.back * UM + d.ssm * US + u

        def pool_c(d, u):
            first = d.back if isinstance(d.back, int) and d.back < len(FIRST_C) else len(FIRST_C)
            rows = sum(UM - UM // c for c in FIRST_C[:first]) + (d.back - first) * (UM - UM // DVE_C)
            return rows + u + 1 - (u + 1) // dve_c(d.back)

        def count(n):
            if isinstance(n, int):
                return max(n, 0)
            assert n.min_val > 0, n
            return n

        def counts(eng, *values):
            return [n if isinstance(n, int) else eng.to_reg(n) for n in map(count, values)]

        def schedule(eng, piece, head=None, tile=None, middle=None, norm=None, steps=None):
            def slot(layer, d, former, parts):
                if head:
                    head(layer, d, former)
                plan = spread(TILES[layer], *parts)
                for t in range(TILES[layer]):
                    if tile:
                        tile(layer, d, t)
                    between = len(plan[t]) // 2 if middle else 0
                    for dd, name, n in plan[t][:between]:
                        piece(dd, name, n)
                    if middle:
                        middle(layer, d, t)
                    for dd, name, n in plan[t][between:]:
                        piece(dd, name, n)

            def alone(layer, d):
                if norm:
                    norm(layer, d)

            start = at(Done(0, 0, 0, 0, 0), FRONT) + at(Done(1, 0, 0, 0, 0), BACK)
            for k, (d, name, n) in enumerate(start):
                piece(d, name, n)
                for j in range(max(k - 1, 0) * (SPLITS + 1) // SPLIT_OVER,
                               min(k * (SPLITS + 1) // SPLIT_OVER, SPLITS + 1)):
                    piece(d, "split", j)
            def ssm_and_mamba(d, behind):
                scan = at(behind._replace(front=d.front + 1), BACK[:EARLY])
                return [(at(d, SSM[:UP_TO_DELTA]), 0, 2), (at(d, SSM[UP_TO_DELTA:]), 4, SSM_END),
                        (at(behind, FRONT[:UP_TO_U]), SSM_END, FRONT_END),
                        (merge(at(behind, FRONT[UP_TO_U:]), scan), FRONT_END, T0)]

            first, second = Done(2, 2, 0, 0, 0), Done(2, 2, 0, 1, 0)
            slot(0, first, None, [(at(Done(1, 1, 0, 0, 0), FRONT), 0, 7),
                                  (at(Done(2, 1, 0, 0, 0), BACK[:BACK_END]), 7, T0)])
            alone(0, first)
            for name, n in BACK[BACK_END:]:
                piece(Done(2, 1, 0, 1, 0), name, n)
            slot(0, second, None, ssm_and_mamba(second, second._replace(ssm=1)))

            def ffn1_and_scan(i):
                d = Done(i + 2, i + 1, i, i + 1, i - 1)
                slot(1, d, (0, d._replace(f0=i)), [(at(d, BACK[EARLY:UM + Y_LAG]), 0, T1 - TAIL),
                                                   (at(d, BACK[UM + Y_LAG:]), T1 - TAIL, T1)])

            def ffn0_and_ssm(i):
                d = Done(i + 2, i + 2, i, i + 1, i)
                slot(0, d, (1, d._replace(f1=i - 1)), ssm_and_mamba(d, d._replace(ssm=i + 1)))

            with eng.Fori(1, BATCH - 2) as i:
                if steps:
                    steps.loop(i)
                ffn1_and_scan(i)
                ffn0_and_ssm(i)
            if steps:
                steps.behind()
            ffn1_and_scan(BATCH - 2)
            d = Done(BATCH, BATCH, BATCH - 2, BATCH - 1, BATCH - 2)
            slot(0, d, (1, d._replace(f1=BATCH - 3)), [(at(d, SSM), 0, T0)])
            d = Done(BATCH, BATCH, BATCH - 1, BATCH, BATCH - 2)
            slot(1, d, (0, d._replace(f0=BATCH - 1)), [(at(d, SSM[:SSM_LAST]), 0, T1)])
            alone(1, d)
            d = d._replace(f1=BATCH - 1)
            for name, n in SSM[SSM_LAST:]:
                piece(d, name, n)
            slot(1, d, None, [])
            alone(1, d)

        ctx.enter_context(nc.allow_non_contiguous_dma(reason="rows sent to all partitions"))
        block = ctx.enter_context(nc.Block())

        @block.sync
        def _(sp):
            sp.dma_start(par[:], params).then_inc(par_loaded, 16)
            sp.dma_start(sel_sb[:], sel).then_inc(par_loaded, 16)

            to_store = []

            def load_x(d):
                at = d.front * L
                if not isinstance(at, int):
                    at = sp.snap(at)
                sp.wait_ge(x_ready[0], count(d.back))
                sp.dma_start(x_in[:], xT[:, :, bass.ds(at, L)]).then_inc(x_loaded, 16)

            def rows_of(src, g):
                rows = src[g * NS:(g + 1) * NS, :].rearrange("n l -> (n l)")
                return rows.partition_broadcast(P)

            def load_rows(d, what, g):
                slot, former = g % BC_RING, g - BC_RING
                used = 0 if former < 0 else (former // 2) * 2 * CB + 2 * CB - 1 + former % 2
                if what == "b":
                    bc_stored_n, bx_done_n = counts(sp, 16 * (d.back + 1), units(d, used))
                    sp.wait_ge(bc_stored, bc_stored_n)
                    sp.wait_ge(bx_done, bx_done_n)
                    sp.dma_start(b_bc[:, slot], rows_of(bc_dram[0:NST, :], g)).then_inc(b_loaded[slot], 16)
                else:
                    x_ready_n, y_added_n = counts(sp, d.ssm, d.back * UM + used)
                    sp.wait_ge(x_ready[2], x_ready_n)
                    sp.wait_ge(y_added, y_added_n)
                    sp.dma_start(c_bc[:, slot], rows_of(bc_dram[NST:2 * NST, :], g)).then_inc(c_loaded[slot], 16)

            def load_delta(d, g):
                slot, former = g % BC_RING, g - BC_RING
                dl_stored_n, bx_done_n = counts(sp, 16 * (d.ssm + 1), units(d, max(KD * (former + 1), 0)))
                sp.wait_ge(dl_stored, dl_stored_n)
                sp.wait_ge(bx_done, bx_done_n)
                sp.dma_start(b_bc[:, slot], rows_of(dl_dram, g)).then_inc(b_loaded[slot], 16)

            def load_gu(layer, d, t):
                slot = t % W_RING
                sp.wait_ge(gu_filled, count(ffn_count(d, 1) + t - W_RING + 1))
                sp.dma_start(gu_ring[:, slot].bitcast(F32), gu_dram[layer * T0 + t]).then_inc(gu_loaded[slot], 16)

            def load_down(layer, d, t):
                slot = t % W_RING
                sp.wait_ge(tile_done, count(ffn_count(d, 1) + t - W_RING + 1))
                sp.dma_start(down_ring[:, slot], down_w[layer * T0 + t]).then_inc(down_loaded[slot], 16)

            def load_raw(j):
                sp.wait_ge(w_low, count(j - 1))
                sp.dma_start(raw[j % 2], gu_w[2 * j:2 * j + 2].rearrange("t p (b l) -> p t b l", b=1)).then_inc(
                    raw_loaded[j % 2], 16)

            def store_split(j):
                sp.wait_ge(w_low, j + 1)
                half = j % 2
                sp.dma_start(gu_dram[2 * j:2 * j + 2].rearrange("t p h n -> p t h n"),
                             gu_ring[:, 2 * half:2 * half + 2].bitcast(F32)).then_inc(split_stored[half], 16)

            def store(d):
                at = d.f1 * L
                if not isinstance(at, int):
                    at = sp.snap(at)
                sp.wait_ge(out_ready, count(d.f1 + 1))
                sp.dma_start(out[:, :, bass.ds(at, L)], pre_f[:]).then_inc(out_stored, 16)

            def piece(d, name, n):
                if (name, n) == ("in", 0):
                    load_x(d)
                elif name == "split":
                    if n < SPLITS:
                        load_raw(n)
                    if n >= 1:
                        store_split(n - 1)
                elif (name, n) in ROWS:
                    what, g = ROWS[name, n]
                    load_rows(d, what, int(g))
                elif name == "s_unit" and n == 0:
                    load_delta(d, 0)
                    load_delta(d, 1)
                elif name == "s_unit" and n in (1, 2):
                    load_delta(d, n + 1)
                elif name == "s_unit" and n % KD == 1 and BC_RING <= BC_RING + n // KD - 2 < GROUPS:
                    load_delta(d, BC_RING + n // KD - 2)

            def head(layer, d, former):
                if isinstance(d.f0, int) and d.f0 == 0:
                    for half in range(2):
                        sp.wait_ge(split_stored[half], 16 * (SPLITS // 2))
                for t in range(W_RING):
                    load_gu(layer, d, t)
                for t in range(DOWN_AHEAD):
                    load_down(layer, d, t)
                if former and former[0]:
                    to_store.append(former[1])

            def tile(layer, d, t):
                if t == STORE_TILE and to_store:
                    store(to_store.pop())
                if t + DOWN_AHEAD < TILES[layer]:
                    load_down(layer, d, t + DOWN_AHEAD)
                if t + W_RING < TILES[layer]:
                    load_gu(layer, d, t + W_RING)

            def norm(layer, d):
                if layer:
                    store(d)

            schedule(sp, piece, head, tile, None, norm)
            sp.wait_ge(out_stored, 16 * (BATCH + 1))

        @block.gpsimd
        def _(pool):
            nc.gpsimd.memset(mean_w[:], 1.0 / D)
            nc.gpsimd.memset(eps_b[:], EPS).then_inc(out_stored, 16)
            nc.gpsimd.memset(x_pad[:, :, 0:CONV - 1], 0.0)
            nc.gpsimd.memset(d_a[:, :, :, 0:1], 0.0)
            nc.gpsimd.memset(coef_parts[:], 0.0).then_inc(prep_pool, 1)

            def scan_input(d, u, ssm):
                g, c = (u // KD, u % KD) if ssm else mixer_unit(u)
                src = xp[:, c:c + 1] if ssm else xu[:, c:c + 1]
                if u == 0:
                    pool.wait_ge(coef_done, count(d.back + d.ssm))
                    if ssm:
                        pool.wait_ge(mix_drained, count(drained(d, KD)))
                        pool.wait_ge(y_added, count(d.back * UM))
                        pool.wait_ge(x_ready[0], count(d.back))
                    else:
                        pool.wait_ge(u_done, count(d.back + 1))
                        pool.wait_ge(reduced, count(d.ssm * PS))
                        pool.wait_ge(x_ready[2], count(d.ssm))
                pool.wait_ge(b_loaded[g % BC_RING],
                             count(16 * ((d.back + d.ssm) * (GROUPS // BC_RING) + g // BC_RING + 1)))
                if ssm:
                    pool.wait_ge(reduced, count(d.ssm * PS + u // KD - 1))
                else:
                    pool.wait_ge(y_added, count(d.back * UM + u - H_RING + 1))
                nc.gpsimd.tensor_tensor(h_buf[:, u % H_RING], src.to_broadcast([P, NS, L]),
                                        b_bc[:, g % BC_RING], ALU.mult).then_inc(bx_done, 1)

            def times_c(d, u):
                g, _ = mixer_unit(u)
                pool.wait_ge(scanned, count(units(d, u + 1)))
                pool.wait_ge(c_loaded[g % BC_RING], count(16 * (d.back * (GROUPS // BC_RING) + g // BC_RING + 1)))
                h = h_buf[:, u % H_RING]
                nc.gpsimd.tensor_tensor(h, h, c_bc[:, g % BC_RING], ALU.mult).then_inc(hc_done, 1)

            def piece(d, name, n):
                if name == "unit":
                    for u in ahead(n):
                        scan_input(d, u, False)
                    if 1 <= n <= UM and not on_dve(d.back, n - 1):
                        times_c(d, n - 1)
                elif name == "s_unit" and n < US:
                    scan_input(d, n, True)

            schedule(pool, piece)

        @block.scalar
        def _(act):
            steps = Steps(ACT_STEPS)

            def link(ins):
                ins.then_inc(act_step, 1)
                act.wait_ge(act_step, count(steps.next()))

            act.wait_ge(par_loaded, 32)
            nc.scalar.activation(neg_a[:], a_log, ACT.Exp).then_inc(prep_act, 1)
            nc.scalar.activation(decay[:], a_s, ACT.Exp, scale=-1.0).then_inc(prep_act, 1)
            act.wait_ge(prep_pool, 1)
            act.wait_ge(prep_dve, 3)

            def conv_input(d, m):
                act.wait_ge(mix_filled, count(filled(d, F_X + m)))
                act.wait_ge(conv_done, count(d.front * CB + m - 1))
                nc.scalar.copy(x_pad[:, m % 2, CONV - 1:], mix_ps[:]).then_inc(mix_drained, 1)

            def conv_tanh(d, m):
                act.wait_ge(conv_done, count(d.front * CB + m + 1))
                act.wait_ge(silu_done, count(d.front * 2 * CB + m - 1))
                nc.scalar.activation(tanh_m[:, m % 2], half_x[:, m % 2], ACT.Tanh).then_inc(tanh_done, 1)

            def rows_out(d):
                act.wait_ge(mix_filled, count(filled(d, F_XP)))
                act.wait_ge(bc_stored, count(16 * d.front))
                nc.scalar.copy(x_dbl[:], mix_ps[0:XD, :]).then_inc(mix_drained, 1)
                act.wait_ge(mix_drained, count(drained(d, F_XP + 1)))
                act.wait_ge(y_added, count(d.back * UM))
                act.dma_start(bc_dram, x_dbl[RANK:XD, :]).then_inc(bc_stored, 16)

            def delta_in(d, m):
                act.wait_ge(mix_filled, count(filled(d, F_DT + m)))
                act.wait_ge(da_done, count(d.back * UM))
                nc.scalar.activation(delta[:, m], mix_ps[:], ACT.Identity,
                                     bias=dt_b[:, m:m + 1]).then_inc(mix_drained, 1)

            def softplus(d, n):
                if n == 0:
                    act.wait_ge(mix_drained, count(drained(d, F_DT + CB)))
                    link(nc.scalar.activation(y[:], delta[:], ACT.Abs))
                elif n == 1:
                    link(nc.scalar.activation(y[:], y[:], ACT.Exp, scale=-1.0))
                else:
                    nc.scalar.activation(y[:], y[:], ACT.Ln, bias=1.0).then_inc(softplus_log, 1)

            def z_in(d, m):
                act.wait_ge(mix_filled, count(filled(d, F_Z + m)))
                act.wait_ge(silu_done, count(d.front * 2 * CB + CB + m - 1))
                nc.scalar.activation(tanh_m[:, m % 2], mix_ps[:], ACT.Tanh, scale=0.5).then_inc(tanh_done, 1)
                nc.scalar.activation(z_act[:, m], mix_ps[:], ACT.Copy, scale=0.5).then_inc(mix_drained, 1)

            def decays(d, u):
                g, c = mixer_unit(u)
                act.wait_ge(delta_done, count(d.back + 1))
                act.wait_ge(scanned, count(units(d, u - DA_RING + 1)))
                for j in range(NS):
                    last = nc.scalar.activation(d_a[:, u % DA_RING, j, 1:L], delta[:, c, 1:L], ACT.Exp,
                                                scale=neg_a[:, c, g * NS + j:g * NS + j + 1])
                last.then_inc(da_done, 1)

            def square(centered):
                act.wait_ge(mix_drained, count(centered))
                nc.scalar.activation(sq, pre, ACT.Square).then_inc(squared, 1)

            def inv_std(variance, n):
                act.wait_ge(mix_filled, count(variance))
                nc.scalar.activation(rstd, mix_ps[:], ACT.Ln, bias=eps_b[:]).then_inc(mix_drained, 1)
                act.wait_ge(mix_drained, count(n))
                nc.scalar.activation(rstd, rstd, ACT.Exp, scale=-0.5).then_inc(rstd_done, 1)

            def ssm_delta(d):
                act.wait_ge(mix_filled, count(filled(d, S_DL)))
                nc.scalar.copy(sp_v, mix_ps[0:NST, :]).then_inc(mix_drained, 1)
                act.wait_ge(mix_drained, count(drained(d, S_DL + 1)))
                link(nc.scalar.activation(sp_a, sp_v, ACT.Abs))
                link(nc.scalar.activation(sp_a, sp_a, ACT.Exp, scale=-1.0))
                nc.scalar.activation(sp_a, sp_a, ACT.Ln, bias=1.0).then_inc(s_log, 1)

            def split_high(j):
                act.wait_ge(raw_loaded[j % 2], 16 * (j // 2 + 1))
                act.wait_ge(split_stored[j % 2], 16 * (j // 2))
                half = 2 * (j % 2)
                nc.scalar.activation(gu_ring[:, half:half + 2, 0:1], raw[j % 2], ACT.Copy).then_inc(w_high, 1)

            def piece(d, name, n):
                if name == "split" and n < SPLITS:
                    split_high(n)
                elif name == "in":
                    if n < CB:
                        conv_input(d, n)
                    if n >= 1:
                        conv_tanh(d, n - 1)
                elif name == "x_proj":
                    rows_out(d)
                elif name == "dt":
                    delta_in(d, n)
                elif name == "softplus":
                    softplus(d, n)
                elif name == "z" and n < CB:
                    z_in(d, n)
                elif name == "unit":
                    for u in ahead(n):
                        decays(d, u)
                elif name == "b_mean":
                    square(drained(d, B_MEAN + 1))
                elif name == "b_var":
                    inv_std(filled(d, B_VAR), drained(d, B_VAR + 1))
                elif name == "xp":
                    act.wait_ge(mix_filled, count(filled(d, S_XP + n, True)))
                    act.wait_ge(y_added, count(d.back * UM))
                    nc.scalar.activation(xp[:, n], mix_ps[:], ACT.Identity,
                                         bias=b_pin[:, n:n + 1]).then_inc(mix_drained, 1)
                elif name == "s_delta":
                    ssm_delta(d)
                elif name == "s_plus":
                    act.wait_ge(s_delta, count(d.ssm + 1))
                    act.wait_ge(bx_done, count(units(d)))
                    act.dma_start(dl_dram, sp_d).then_inc(dl_stored, 16)
                elif name == "c_y" and n == 0:
                    act.wait_ge(reduced, count((d.ssm + 1) * PS))
                    nc.scalar.copy(h_sum, mix_ps[0:NST, :]).then_inc(mix_drained, 1)
                elif name == "s_out":
                    act.wait_ge(mix_filled, count(filled(d, S_PO + n, True)))
                    nc.scalar.activation(pre[:, n], mix_ps[:], ACT.Identity,
                                         bias=b_pout[:, n:n + 1]).then_inc(mix_drained, 1)
                elif name == "s_mean":
                    square(drained(d, S_MEAN + 1))
                elif name in ("route0", "route1") and n == 2:
                    router_exp(int(name == "route1"), d)
                elif name == "s_var":
                    inv_std(filled(d, S_VAR, True), drained(d, S_VAR + 1))

            def router_exp(layer, d):
                e = E1 if layer else E0
                act.wait_ge(shifted, count(d.back + d.ssm + 1))
                if layer == 0:
                    nc.scalar.activation(prob[:, :, E0:], logits[:, :, E0:], ACT.Tanh, scale=0.5)
                nc.scalar.activation(prob[:, :, 0:e], coef[:, :, 0:e], ACT.Exp).then_inc(prob_done, 1)

            def gate_tanh(layer, d, t):
                act.wait_ge(gu_filled, count(ffn_count(d, 1) + t + 1))
                act.wait_ge(gu_drained, count(ffn_count(d, 1) + t - 1))
                nc.scalar.activation(tanh_g[:, t % 2], gate_ps[t % 2][:], ACT.Tanh,
                                     scale=0.5).then_inc(tanh_g_done, 1)

            def norm_square(n):
                act.wait_ge(norm_drained, count(2 * n - 1))
                nc.scalar.activation(sq_f[:], pre_f[:], ACT.Square).then_inc(squared_f, 1)

            def norm_inv_std(n):
                act.wait_ge(norm_filled, count(2 * n))
                nc.scalar.activation(rstd_f[:], out_ps[1][:], ACT.Ln, bias=eps_b[:]).then_inc(norm_drained, 1)
                act.wait_ge(norm_drained, count(2 * n))
                nc.scalar.activation(rstd_f[:], rstd_f[:], ACT.Exp, scale=-0.5).then_inc(rstd_f_done, 1)

            def head(layer, d, former):
                act.wait_ge(x_ready[2 * layer], count((d.f1 if layer else d.f0) + 1))
                act.wait_ge(gu_filled, count(ffn_count(d, 1)))
                nc.scalar.activation(x_parts[:, 0], xs[2 * layer][:], ACT.Copy).then_inc(x_high, 1)
                if former:
                    norm_square(d.f0 + d.f1)
                gate_tanh(layer, d, 0)
                if former:
                    norm_inv_std(d.f0 + d.f1)

            def tile(layer, d, t):
                if t + 1 < TILES[layer]:
                    gate_tanh(layer, d, t + 1)

            def norm(layer, d):
                norm_square(d.f0 + d.f1 + 1)
                norm_inv_std(d.f0 + d.f1 + 1)

            schedule(act, piece, head, tile, None, norm, steps)

        @block.vector
        def _(dve):
            steps = Steps(DVE_STEPS)

            def link(ins):
                ins.then_inc(dve_step, 1)
                dve.wait_ge(dve_step, count(steps.next()))

            dve.wait_ge(par_loaded, 32)
            nc.vector.tensor_scalar_mul(half_cw[:], conv_w, 0.5)
            nc.vector.tensor_scalar_mul(half_cb[:], conv_b, 0.5)
            dve.wait_ge(prep_act, 2)
            nc.vector.tensor_scalar_add(decay[:], decay[:], 1.0).then_inc(prep_dve, 1)
            dve.wait_ge(prep_dve, 1)
            nc.vector.reciprocal(decay[:], decay[:]).then_inc(prep_dve, 1)
            dve.wait_ge(prep_dve, 2)
            nc.vector.tensor_scalar_mul(neg_a[:], neg_a[:], -1.0).then_inc(prep_dve, 1)
            dve.wait_ge(prep_dve, 3)
            dve.wait_ge(prep_pool, 1)

            def on_blocks(a):
                return a.rearrange("p (a l) -> p a l", a=1).to_broadcast([P, KD, L])

            def flat(a):
                return a.rearrange("p a l -> p (a l)")

            def convolve(d, m):
                mix_drained_n, silu_done_n = counts(dve, drained(d, F_X + m + 1), d.front * 2 * CB + m - 1)
                dve.wait_ge(mix_drained, mix_drained_n)
                dve.wait_ge(silu_done, silu_done_n)
                h, x = half_x[:, m % 2], x_pad[:, m % 2]
                tap = nc.vector.tensor_scalar(h, x[:, CONV - 1:], half_cw[:, m, CONV - 1:], half_cb[:, m:m + 1],
                                              ALU.mult, ALU.add)
                for k in range(CONV - 2, -1, -1):
                    link(tap)
                    tap = nc.vector.scalar_tensor_tensor(h, x[:, k:k + L], half_cw[:, m, k:k + 1], h,
                                                         ALU.mult, ALU.add)
                tap.then_inc(conv_done, 1)

            def conv_silu(d, m):
                conv_done_n, tanh_done_n, bx_done_n = counts(
                    dve, d.front * CB + m + 1, d.front * 2 * CB + m + 1, units(d))
                dve.wait_ge(conv_done, conv_done_n)
                dve.wait_ge(tanh_done, tanh_done_n)
                dve.wait_ge(bx_done, bx_done_n)
                nc.vector.scalar_tensor_tensor(xu[:, m], tanh_m[:, m % 2], 1.0, half_x[:, m % 2],
                                               ALU.add, ALU.mult).then_inc(silu_done, 1)

            def delta_and_u(d, n):
                if n == 0:
                    dve.wait_ge(softplus_log, count(d.front + 1))
                    nc.vector.scalar_tensor_tensor(flat(delta[:]), flat(delta[:]), 0.0, flat(y[:]),
                                                   ALU.max, ALU.add).then_inc(delta_done, 1)
                elif n == 1:
                    dve.wait_ge(delta_done, count(d.front + 1))
                    for m in range(CB):
                        last = nc.vector.tensor_scalar(y[:, m], xu[:, m], d_m[:, m:m + 1], None, ALU.mult)
                    link(last)
                else:
                    dve.wait_ge(mix_filled, count(filled(d, F_XP)))
                    nc.vector.tensor_tensor(xu[:], xu[:], delta[:], ALU.mult).then_inc(u_done, 1)

            def z_silu(d, m):
                tanh_done_n, mix_drained_n = counts(dve, d.front * 2 * CB + CB + m + 1, drained(d, F_Z + m + 1))
                dve.wait_ge(tanh_done, tanh_done_n)
                dve.wait_ge(mix_drained, mix_drained_n)
                nc.vector.scalar_tensor_tensor(z_act[:, m], tanh_m[:, m % 2], 1.0, z_act[:, m],
                                               ALU.add, ALU.mult).then_inc(silu_done, 1)

            def scan(d, u):
                bx_done_n, da_done_n = counts(dve, units(d, u + 1), d.back * UM + u + 1)
                dve.wait_ge(bx_done, bx_done_n)
                dve.wait_ge(da_done, da_done_n)
                h = flat(h_buf[:, u % H_RING])
                nc.vector.tensor_tensor_scan(h, flat(d_a[:, u % DA_RING]), h, 0.0,
                                             ALU.mult, ALU.add).then_inc(scanned, 1)

            def add_y(d, u):
                g, c = mixer_unit(u)
                h = h_buf[:, u % H_RING]
                if on_dve(d.back, u):
                    scanned_n, c_loaded_n = counts(
                        dve, units(d, u + 1), 16 * (d.back * (GROUPS // BC_RING) + g // BC_RING + 1))
                    dve.wait_ge(scanned, scanned_n)
                    dve.wait_ge(c_loaded[g % BC_RING], c_loaded_n)
                    nc.vector.tensor_tensor(h, h, c_bc[:, g % BC_RING], ALU.mult).then_inc(dve_step, 1)
                    product, former = counts(dve, steps.next(), d.back * UM + u)
                    dve.wait_ge(dve_step, product)
                else:
                    product, former = counts(dve, pool_c(d, u), d.back * UM + u)
                    dve.wait_ge(hc_done, product)
                dve.wait_ge(y_added, former)
                for j in range(NS):
                    last = nc.vector.tensor_tensor(y[:, c], y[:, c], h[:, j], ALU.add)
                    if j < NS - 1:
                        link(last)
                last.then_inc(y_added, 1)

            def gate_y(d):
                y_added_n, silu_done_n = counts(dve, (d.back + 1) * UM, (d.back + 1) * 2 * CB)
                dve.wait_ge(y_added, y_added_n)
                dve.wait_ge(silu_done, silu_done_n)
                nc.vector.tensor_tensor(y[:], y[:], z_act[:], ALU.mult).then_inc(y_gated, 1)

            def residual(d, m):
                dve.wait_ge(mix_filled, count(filled(d, B_OUT + m)))
                nc.vector.tensor_tensor(pre[:, m], mix_ps[:], x_in[:, m], ALU.add).then_inc(mix_drained, 1)

            def center(mean_filled, signal, n):
                mix_filled_n, signal_n = counts(dve, mean_filled, n)
                dve.wait_ge(mix_filled, mix_filled_n)
                dve.wait_ge(signal, signal_n)
                nc.vector.tensor_tensor(pre, pre, on_blocks(mix_ps[:]), ALU.subtract).then_inc(mix_drained, 1)

            def scale(d, dst, ready):
                rstd_done_n, out_drained_n = counts(dve, d.back + d.ssm + 1, d.f0 + d.f1)
                dve.wait_ge(rstd_done, rstd_done_n)
                dve.wait_ge(out_drained, out_drained_n)
                nc.vector.tensor_tensor(dst[:], pre, on_blocks(rstd), ALU.mult).then_inc(ready, 1)

            def ssm_scan(d, u):
                h, g, c = h_buf[:, u % H_RING], u // KD, u % KD
                dve.wait_ge(bx_done, count(units(d, u + 1)))
                for j in range(NS):
                    s = g * NS + j
                    last = nc.vector.tensor_tensor_scan(h[:, j], decay[:, c, s:s + 1].to_broadcast([P, L]),
                                                        h[:, j], 0.0, ALU.mult, ALU.add)
                last.then_inc(scanned, 1)
                if c == KD - 1:
                    dve.wait_ge(scanned, count(units(d, u + 1)))
                    nc.vector.tensor_tensor(h, h, h_buf[:, (u - 1) % H_RING], ALU.add).then_inc(paired, 1)

            def piece(d, name, n):
                if name == "split" and n < SPLITS:
                    dve.wait_ge(w_high, n + 1)
                    half = 2 * (n % 2)
                    high = gu_ring[:, half:half + 2, 0:1].bitcast(F32)
                    nc.vector.tensor_tensor(gu_ring[:, half:half + 2, 1:2], raw[n % 2], high,
                                            ALU.subtract).then_inc(w_low, 1)
                elif name == "in":
                    if n < CB:
                        convolve(d, n)
                    if n >= 1:
                        conv_silu(d, n - 1)
                elif name == "u_y":
                    delta_and_u(d, n)
                elif name == "z" and n >= 1:
                    z_silu(d, n - 1)
                elif name == "unit":
                    if n >= Y_LAG:
                        add_y(d, n - Y_LAG)
                    if n < UM:
                        scan(d, n)
                elif name == "out":
                    if n == 0:
                        gate_y(d)
                    else:
                        residual(d, n - 1)
                elif name == "b_mean":
                    center(filled(d, B_MEAN), mix_drained, drained(d, B_OUT + KD))
                elif name == "b_norm":
                    scale(d, xs[0], x_ready[0])
                elif name == "s_plus":
                    dve.wait_ge(s_log, count(d.ssm + 1))
                    nc.vector.scalar_tensor_tensor(sp_d, sp_v, 0.0, sp_a, ALU.max, ALU.add).then_inc(s_delta, 1)
                elif name == "s_unit" and 1 <= n <= US:
                    ssm_scan(d, n - 1)
                elif name == "c_y":
                    dve.wait_ge(mix_filled, count(filled(d, S_YC + n, True)))
                    nc.vector.scalar_tensor_tensor(ys[:, n], xp[:, n], d_s[:, n:n + 1], mix_ps[:],
                                                   ALU.mult, ALU.add).then_inc(mix_drained, 1)
                elif name == "s_mean":
                    dve.wait_ge(mix_drained, count(drained(d, S_PO + KD)))
                    nc.vector.scalar_tensor_tensor(flat(pre), flat(xs[1][:]), 2.0, flat(pre),
                                                   ALU.mult, ALU.add).then_inc(ssm_pre, 1)
                    center(filled(d, S_MEAN, True), ssm_pre, d.ssm + 1)
                elif name == "s_norm":
                    scale(d, xs[2], x_ready[2])
                elif name in ("route0", "route1"):
                    router(int(name == "route1"), d, n)

            def router(layer, d, n):
                e, k = (E1, K1) if layer else (E0, K0)
                width = e if layer else e + 1
                fill = S_ROUTE if layer else B_ROUTE
                lg, rk = logits[:, :, 0:e], rank[:, :, 0:e]
                pr, cf = prob[:, :, 0:e], coef[:, :, 0:e]
                gt, eq = (flat(a)[:, 0:TT * e * e].rearrange("p (t i j) -> p t i j", t=TT, i=e)
                          for a in (greater, equal))
                if n == 1:
                    dve.wait_ge(mix_filled, count(filled(d, fill, layer == 1)))
                    nc.vector.tensor_copy(logits[:, :, 0:width], mix_ps[:, 0:TT * width].rearrange(
                        "p (t e) -> p t e", t=TT)).then_inc(mix_drained, 1)
                    dve.wait_ge(mix_drained, count(drained(d, fill + 1)))
                    link(nc.vector.tensor_reduce(top[:], lg, AX.X, ALU.max))
                    nc.vector.tensor_tensor(cf, lg, top[:].rearrange("p (t a) -> p t a", a=1).to_broadcast(
                        [P, TT, e]), ALU.subtract).then_inc(shifted, 1)
                elif n == 2:
                    lj = lg.unsqueeze(2).to_broadcast([P, TT, e, e])
                    li = lg.unsqueeze(3).to_broadcast([P, TT, e, e])
                    nc.vector.tensor_tensor(gt, lj, li, ALU.is_gt)
                    link(nc.vector.tensor_tensor(eq, lj, li, ALU.is_equal))
                elif n == 3:
                    lower = before[:, 0:e, 0:e].unsqueeze(1).to_broadcast([P, TT, e, e])
                    link(nc.vector.tensor_tensor(eq, eq, lower, ALU.mult))
                    link(nc.vector.tensor_tensor(gt, gt, eq, ALU.add))
                    link(nc.vector.tensor_reduce(rk, gt, AX.X, ALU.add))
                elif n == 4:
                    dve.wait_ge(prob_done, count(d.back + d.ssm + 1))
                    if layer == 0:
                        nc.vector.tensor_scalar(coef[:, :, E0:], prob[:, :, E0:], 0.25, 0.25, ALU.mult, ALU.add)
                    link(nc.vector.scalar_tensor_tensor(cf, rk, float(k), pr, ALU.is_lt, ALU.mult))
                    link(nc.vector.tensor_reduce(top[:], cf if layer else pr, AX.X, ALU.add))
                    link(nc.vector.reciprocal(inv[:], top[:]))
                    nc.vector.scalar_tensor_tensor(
                        cf, cf, 0.5, inv[:].rearrange("p (t a) -> p t a", a=1).to_broadcast([P, TT, e]),
                        ALU.mult, ALU.mult).then_inc(coef_done, 1)

            def split_coef(layer, d):
                width = E1 if layer else E0 + 1
                dve.wait_ge(side_filled, count(side_count(d) + 1))
                hi, ct = coef_parts[0:width, :], side_ps[0:width, :]
                r, md = rest[0:width, :], mid[0:width, :]
                link(nc.vector.tensor_copy(hi, ct))
                link(nc.vector.tensor_tensor(r, ct, hi, ALU.subtract))
                link(nc.vector.tensor_copy(md, r))
                nc.vector.tensor_copy(coef_parts[EPART:EPART + width, :], md)
                nc.vector.tensor_tensor(coef_parts[2 * EPART:2 * EPART + width, :], r, md,
                                        ALU.subtract).then_inc(side_drained, 1)

            def gate_up(layer, d, t):
                dve.wait_ge(tanh_g_done, count(ffn_count(d, 1) + t + 1))
                silu2 = tanh_g[:, t % 2]
                nc.vector.scalar_tensor_tensor(silu2, silu2, 1.0, gate_ps[t % 2][:],
                                               ALU.add, ALU.mult).then_inc(dve_step, 1)
                dve_step_n, side_drained_n = counts(dve, steps.next(), side_count(d) + 1 + max(t - 1, 0))
                dve.wait_ge(dve_step, dve_step_n)
                dve.wait_ge(side_drained, side_drained_n)
                nc.vector.tensor_tensor(gated_u[:, t % 2], up_ps[t % 2][:], silu2, ALU.mult).then_inc(
                    gu_drained, 1)

            def weight_hidden(layer, d, t):
                side_filled_n, gu_drained_n, tile_done_n = counts(
                    dve, side_count(d) + 2 + t, ffn_count(d, 1) + t + 1, ffn_count(d, 1) + t - 1)
                dve.wait_ge(side_filled, side_filled_n)
                dve.wait_ge(gu_drained, gu_drained_n)
                dve.wait_ge(tile_done, tile_done_n)
                nc.vector.tensor_tensor(hid[:, t % 2], side_ps[:], gated_u[:, t % 2], ALU.mult).then_inc(
                    side_drained, 1)

            def ffn_residual(layer, d):
                tile_done_n, out_stored_n = counts(dve, ffn_count(d, 1) + TILES[layer], 16 * (d.f1 + 1))
                dve.wait_ge(tile_done, tile_done_n)
                dve.wait_ge(out_stored, out_stored_n)
                for m in range(KD):
                    last = nc.vector.tensor_tensor(pre_f[:, m], out_ps[m][:], xs[2 * layer][:, m], ALU.add)
                last.then_inc(out_drained, 1)

            def norm_center(n):
                norm_filled_n, out_drained_n = counts(dve, 2 * n - 1, n)
                dve.wait_ge(norm_filled, norm_filled_n)
                dve.wait_ge(out_drained, out_drained_n)
                nc.vector.tensor_tensor(pre_f[:], pre_f[:], on_blocks(out_ps[0][:]),
                                        ALU.subtract).then_inc(norm_drained, 1)

            def norm_scale(layer, n, ssms):
                rstd_f_done_n, ssm_pre_n = counts(dve, n, ssms)
                dve.wait_ge(rstd_f_done, rstd_f_done_n)
                dve.wait_ge(ssm_pre, ssm_pre_n)
                dst, ready = (pre_f, out_ready) if layer else (xs[1], x_ready[1])
                nc.vector.tensor_tensor(dst[:], pre_f[:], on_blocks(rstd_f[:]), ALU.mult).then_inc(ready, 1)

            def head(layer, d, former):
                dve.wait_ge(x_high, count(d.f0 + d.f1 + 1))
                nc.vector.tensor_tensor(x_parts[:, 1], xs[2 * layer][:], x_parts[:, 0].bitcast(F32),
                                        ALU.subtract).then_inc(x_low, 1)
                if former:
                    ffn_residual(*former)
                split_coef(layer, d)
                if former:
                    norm_center(d.f0 + d.f1)
                gate_up(layer, d, 0)
                if former:
                    norm_scale(former[0], d.f0 + d.f1, d.ssm)

            def tile(layer, d, t):
                weight_hidden(layer, d, t)
                if t + 1 < TILES[layer]:
                    gate_up(layer, d, t + 1)

            def norm(layer, d):
                n = d.f0 + d.f1 + 1
                ffn_residual(layer, d)
                norm_center(n)
                norm_scale(layer, n, 0)

            schedule(dve, piece, head, tile, None, norm, steps)

        @block.tensor
        def _(pe):
            pe.wait_ge(par_loaded, 32)
            pe.wait_ge(prep_pool, 1)

            def project(w, lo, src, blocks, rows=P):
                for k in range(blocks):
                    last = nc.tensor.matmul(mix_ps[0:rows, :], w[:, k, lo:lo + rows], src[:, k],
                                            start=(k == 0), stop=(k == blocks - 1))
                return last

            def mean(src, bank):
                for k in range(KD):
                    last = nc.tensor.matmul(bank[:], mean_w[:], src[:, k], start=(k == 0), stop=(k == KD - 1))
                return last

            def reduce_pair(d, p):
                pe.wait_ge(paired, count(d.ssm * PS + p + 1))
                for j in range(NS):
                    s = p * NS + j
                    last = nc.tensor.matmul(mix_ps[0:NST, :], onecol[:, NST - 1 - s:2 * NST - 1 - s],
                                            h_buf[:, (KD * p + KD - 1) % H_RING, j], start=(s == 0),
                                            stop=(s == NST - 1))
                last.then_inc(reduced, 1)

            def route_logits(layer, d):
                x, width = xs[2 * layer], E1 if layer else E0 + 1
                pe.wait_ge(mix_drained, count(drained(d, S_ROUTE if layer else B_ROUTE)))
                pe.wait_ge(x_ready[2 * layer], count((d.ssm if layer else d.back) + 1))
                for tt in range(TT):
                    for k in range(KD):
                        last = nc.tensor.matmul(mix_ps[:, tt * width:(tt + 1) * width],
                                                x[:, k, tt * P:(tt + 1) * P], gates[layer][:, k],
                                                start=(k == 0), stop=(k == KD - 1))
                last.then_inc(mix_filled, 1)

            def piece(d, name, n):
                if name == "in" and n < CB:
                    pe.wait_ge(mix_drained, count(drained(d, F_X + n)))
                    pe.wait_ge(x_loaded, count(16 * (d.front + 1)))
                    project(w_in, n * P, x_in, KD).then_inc(mix_filled, 1)
                elif name == "x_proj":
                    pe.wait_ge(mix_drained, count(drained(d, F_XP)))
                    pe.wait_ge(silu_done, count(d.front * 2 * CB + CB))
                    project(w_x, 0, xu, CB, XD).then_inc(mix_filled, 1)
                elif name == "dt":
                    pe.wait_ge(mix_drained, count(drained(d, F_DT + n)))
                    nc.tensor.matmul(mix_ps[:], w_dt[0:RANK, n * P:(n + 1) * P], x_dbl[0:RANK, :],
                                     start=True, stop=True).then_inc(mix_filled, 1)
                elif name == "z" and n < CB:
                    pe.wait_ge(mix_drained, count(drained(d, F_Z + n)))
                    project(w_in, DI + n * P, x_in, KD).then_inc(mix_filled, 1)
                elif name == "out" and n < KD:
                    pe.wait_ge(mix_drained, count(drained(d, B_OUT + n)))
                    pe.wait_ge(y_gated, count(d.back + 1))
                    project(w_out, n * P, y, CB).then_inc(mix_filled, 1)
                elif name == "b_mean":
                    pe.wait_ge(mix_drained, count(drained(d, B_MEAN)))
                    mean(pre, mix_ps).then_inc(mix_filled, 1)
                elif name == "b_var":
                    pe.wait_ge(mix_drained, count(drained(d, B_VAR)))
                    pe.wait_ge(squared, count(d.back + d.ssm + 1))
                    mean(sq, mix_ps).then_inc(mix_filled, 1)
                elif name in ("route0", "route1") and n == 0:
                    route_logits(int(name == "route1"), d)
                elif name == "xp":
                    pe.wait_ge(mix_drained, count(drained(d, S_XP + n)))
                    pe.wait_ge(x_ready[1], count(d.ssm + 1))
                    project(w_pin, n * P, xs[1], KD).then_inc(mix_filled, 1)
                elif name == "s_delta":
                    pe.wait_ge(mix_drained, count(drained(d, S_DL)))
                    project(w_b, 0, xp, KD, NST).then_inc(mix_filled, 1)
                elif name == "s_unit" and n >= KD + 1 and n % KD == 1:
                    if n == KD + 1:
                        pe.wait_ge(mix_drained, count(drained(d, S_H)))
                    reduce_pair(d, n // KD - 1)
                elif name == "c_y":
                    pe.wait_ge(mix_drained, count(drained(d, S_YC + n)))
                    nc.tensor.matmul(mix_ps[:], c_w[0:NST, n * P:(n + 1) * P], h_sum,
                                     start=True, stop=True).then_inc(mix_filled, 1)
                elif name == "s_out":
                    pe.wait_ge(mix_drained, count(drained(d, S_PO + n)))
                    project(w_pout, n * P, ys, KD).then_inc(mix_filled, 1)
                elif name == "s_mean":
                    pe.wait_ge(mix_drained, count(drained(d, S_MEAN)))
                    pe.wait_ge(ssm_pre, count(d.ssm + 1))
                    mean(pre, mix_ps).then_inc(mix_filled, 1)
                elif name == "s_var":
                    pe.wait_ge(mix_drained, count(drained(d, S_VAR)))
                    pe.wait_ge(squared, count(d.back + d.ssm + 1))
                    mean(sq, mix_ps).then_inc(mix_filled, 1)

            def loads(d, t):
                return d.f0 * (T0 // W_RING) + d.f1 * (T1 // W_RING) + t // W_RING + 1

            def gate_and_up(layer, d, t):
                pe.wait_ge(gu_loaded[t % W_RING], count(16 * loads(d, t)))
                pe.wait_ge(gu_drained, count(ffn_count(d, 1) + t - 1))
                if t == 0:
                    pe.wait_ge(x_low, count(d.f0 + d.f1 + 1))
                high, low = gu_ring[:, t % W_RING, 0], gu_ring[:, t % W_RING, 1]
                for which, bank in ((0, gate_ps[t % 2]), (1, up_ps[t % 2])):
                    for k in range(KD):
                        lo = (which * KD + k) * P
                        for w, part in ((high, 0), (high, 1), (low, 0)):
                            last = nc.tensor.matmul(bank[:], w[:, lo:lo + P], x_parts[:, part, k],
                                                    start=(k == 0 and w is high and part == 0),
                                                    stop=(k == KD - 1 and w is low))
                last.then_inc(gu_filled, 1)

            def down(layer, d, t):
                pe.wait_ge(down_loaded[t % W_RING], count(16 * loads(d, t)))
                pe.wait_ge(side_drained, count(side_count(d) + 2 + t))
                if t == 0:
                    pe.wait_ge(norm_drained, count(2 * (d.f0 + d.f1)))
                w = down_ring[:, t % W_RING]
                for m in range(KD):
                    last = nc.tensor.matmul(out_ps[m][:], w[:, m * P:(m + 1) * P], hid[:, t % 2],
                                            start=(t == 0), stop=(t == TILES[layer] - 1))
                last.then_inc(tile_done, 1)

            def spread_coef(layer, d, t):
                pe.wait_ge(side_drained, count(side_count(d) + 1 + t))
                which = T0 + t // (I1 // P) if layer else t
                nc.tensor.matmul(side_ps[:], sel_sb[:, which], coef_parts[:], start=True,
                                 stop=True).then_inc(side_filled, 1)

            def norm_mean(n):
                pe.wait_ge(out_drained, count(n))
                mean(pre_f, out_ps[0]).then_inc(norm_filled, 1)

            def norm_var(n):
                pe.wait_ge(squared_f, count(n))
                mean(sq_f, out_ps[1]).then_inc(norm_filled, 1)

            def head(layer, d, former):
                width = E1 if layer else E0 + 1
                pe.wait_ge(coef_done, count(d.f0 + d.f1 + 1))
                pe.wait_ge(side_drained, count(side_count(d)))
                for tt in range(TT):
                    last = nc.tensor.matmul(side_ps[0:width, tt * P:(tt + 1) * P], coef[:, tt, 0:width], ident,
                                            start=True, stop=True)
                last.then_inc(side_filled, 1)
                gate_and_up(layer, d, 0)
                if former:
                    norm_mean(d.f0 + d.f1)
                gate_and_up(layer, d, 1)
                if former:
                    norm_var(d.f0 + d.f1)
                spread_coef(layer, d, 0)

            def tile(layer, d, t):
                if t + 2 < TILES[layer]:
                    gate_and_up(layer, d, t + 2)

            def middle(layer, d, t):
                if t >= 1:
                    down(layer, d, t - 1)
                if t + 1 < TILES[layer]:
                    spread_coef(layer, d, t + 1)
                else:
                    down(layer, d, t)

            def norm(layer, d):
                norm_mean(d.f0 + d.f1 + 1)
                norm_var(d.f0 + d.f1 + 1)

            schedule(pe, piece, head, tile, middle, norm)


ACT_STEPS = 4
DVE_STEPS = 127 + UM // DVE_C


def kernel(**inputs):
    import concourse.bacc as bacc
    from concourse.bass_utils import run_bass_kernel_spmd

    a = {k: np.asarray(v) for k, v in inputs.items()}

    def rows(w, blocks):
        n = w.shape[0] // blocks
        return np.ascontiguousarray(w.reshape(blocks, n, -1).transpose(1, 0, 2)).reshape(n, -1)

    def padded(w):
        full = np.zeros((P, w.shape[1]), w.dtype)
        full[:w.shape[0]] = w
        return full

    onecol = np.zeros((P, 2 * NST - 1), np.float32)
    onecol[:, NST - 1] = 1.0
    before = np.broadcast_to(np.tril(np.ones((E0, E0), np.float32), -1).reshape(1, -1), (P, E0 * E0))
    gate0 = np.concatenate([a["L0_ffn_gate_w"], a["L0_ffn_sgate_w"]], 0).T
    values = {
        "w_in": rows(a["L0_attn_in_proj_w"].T, KD), "w_x": rows(a["L0_attn_x_proj_w"].T, CB),
        "w_out": rows(a["L0_attn_out_proj_w"].T, CB), "w_dt": padded(a["L0_attn_dt_proj_w"].T),
        "c_w": padded(a["L1_attn_C_w"].T), "w_pin": rows(a["L1_attn_proj_in_w"].T, KD),
        "w_pout": rows(a["L1_attn_proj_out_w"].T, KD), "w_b": rows(a["L1_attn_B_w"].T, KD),
        "gate0": rows(gate0, KD), "gate1": rows(a["L1_ffn_gate_kernel"], KD),
        "ident": np.eye(P, dtype=np.float32), "onecol": onecol, "conv_w": rows(a["L0_attn_conv_w"], CB),
        "conv_b": rows(a["L0_attn_conv_b"][:, None], CB), "dt_b": rows(a["L0_attn_dt_proj_b"][:, None], CB),
        "a_log": rows(a["L0_attn_A_log"], CB), "d_m": rows(a["L0_attn_D"][:, None], CB),
        "b_pin": rows(a["L1_attn_proj_in_b"][:, None], KD), "b_pout": rows(a["L1_attn_proj_out_b"][:, None], KD),
        "a_s": rows(a["L1_attn_A"], KD), "d_s": rows(a["L1_attn_D_param"][:, None], KD), "before": before,
    }
    params = np.concatenate([values[name] for name, _ in PARAMS], 1)

    def hidden_tiles(gate, up, dn, tiles):
        pad = tiles * P - gate.shape[1]
        g, u = (np.pad(w, ((0, 0), (0, pad))).reshape(KD, P, tiles, P).transpose(2, 1, 0, 3).reshape(
            tiles, P, KD * P) for w in (gate, up))
        return np.concatenate([g, u], 2), np.pad(dn, ((0, pad), (0, 0))).reshape(tiles, P, D)

    w13, w2 = a["L0_ffn_w13"], a["L0_ffn_w2"]
    sgu, sdn = a["L0_ffn_shared_gate_up_w"], a["L0_ffn_shared_down_w"]
    ffn0 = hidden_tiles(np.concatenate([w13[:, :I0].reshape(-1, D), sgu[:IS]], 0).T,
                        np.concatenate([w13[:, I0:].reshape(-1, D), sgu[IS:]], 0).T,
                        np.concatenate([w2.transpose(0, 2, 1).reshape(-1, D), sdn.T], 0), T0)
    ffn1 = hidden_tiles(a["L1_ffn_w0_kernel"].transpose(1, 0, 2).reshape(D, -1),
                        a["L1_ffn_w1_kernel"].transpose(1, 0, 2).reshape(D, -1),
                        a["L1_ffn_wo_kernel"].reshape(-1, D), T1)
    gu_w, down_w = (np.ascontiguousarray(np.concatenate(w, 0)) for w in zip(ffn0, ffn1))

    sel = np.zeros((3 * EPART, T0 + E1, P), np.float32)
    for t in range(T0):
        for i in range(P):
            unit = t * P + i
            expert = unit // I0 if unit < E0 * I0 else E0
            sel[[expert, EPART + expert, 2 * EPART + expert], t, i] = 1.0
    for e in range(E1):
        sel[[e, EPART + e, 2 * EPART + e], T0 + e, :] = 1.0
    sel = sel.astype(mybir.dt.np(BF16))

    xT = np.ascontiguousarray(a["L0_attn_hidden_states"].reshape(BATCH * L, D).T)
    nc = bacc.Bacc("TRN2", target_bir_lowering=False, num_devices=1)
    x_d = nc.dram_tensor("xT", [D, BATCH * L], F32, kind="ExternalInput").ap()
    p_d = nc.dram_tensor("params", [P, NPAR], F32, kind="ExternalInput").ap()
    s_d = nc.dram_tensor("sel", list(sel.shape), BF16, kind="ExternalInput").ap()
    g_d = nc.dram_tensor("gu_w", list(gu_w.shape), F32, kind="ExternalInput").ap()
    w_d = nc.dram_tensor("down_w", list(down_w.shape), F32, kind="ExternalInput").ap()
    o_d = nc.dram_tensor("outT", [D, BATCH * L], F32, kind="ExternalOutput").ap()
    build(nc, x_d.rearrange("(k p) n -> p k n", p=P), p_d, s_d, g_d, w_d, o_d.rearrange("(k p) n -> p k n", p=P))
    arrays = {"xT": xT, "params": params, "sel": sel, "gu_w": gu_w, "down_w": down_w}
    res = run_bass_kernel_spmd(nc, [arrays], core_ids=[0])
    return np.ascontiguousarray(res.results[0]["outT"].T).reshape(BATCH, L, D)
```
